# Optimizing a Trainium2 kernel written in Bass

```python
import numpy as np
import jax
import jax.numpy as jnp

def _softmax(x, axis=-1):
    return jax.nn.softmax(x, axis=axis)

def _gelu(x):
    return jax.nn.gelu(x, approximate=True)

def _silu(x):
    return jax.nn.silu(x)

def _sigmoid(x):
    return jax.nn.sigmoid(x)

def _layernorm(x, axis=-1, eps=1e-05):
    m = jnp.mean(x, axis=axis, keepdims=True)
    v = jnp.var(x, axis=axis, keepdims=True)
    return (x - m) / jnp.sqrt(v + eps)

def _scatter_add(tgt, idx, src, axis=0):
    return tgt.at[idx].add(src)

def _segment_sum(src, seg, n):
    return jax.ops.segment_sum(src, seg, n)
kernel_name = 'mk_adaln_d1_jaxref_r2_9c056e'

def setup_inputs(seed: int=0):
    np.random.seed(seed)
    _w = jnp.asarray

    def _L0_attn_setup():
        import jax, jax.numpy as jnp
        import numpy as np
        B, T, DM = (2, 1024, 512)
        DH = 128
        NH = DM // DH
        ROTARY_BASE = 10000.0

        def fractional_rope(x, base):
            dh = x.shape[-1]
            rot, skip = jnp.split(x, 2, axis=-1)
            width = rot.shape[-1]
            half = width // 2
            t = rot.shape[-2]
            positions = jnp.arange(t)[:, None]
            dims = jnp.arange(half)
            ang_freqs = jnp.power(base, -dims / half)[None, :]
            radians = positions * ang_freqs
            cos = jnp.cos(radians).astype(x.dtype)
            sin = jnp.sin(radians).astype(x.dtype)
            even, odd = jnp.split(rot, 2, axis=-1)
            r_even = even * cos - odd * sin
            r_odd = even * sin + odd * cos
            return jnp.concatenate([r_even, r_odd, skip], axis=-1)
        key = jax.random.key(seed)
        ks = jax.random.split(key, 5)
        scale = (1.0 / DM) ** 0.5
        x = jax.random.normal(ks[0], (B, T, DM), dtype=jnp.float32)
        wq = jax.random.normal(ks[1], (NH, DM, DH), dtype=jnp.float32) * scale
        wk = jax.random.normal(ks[2], (NH, DM, DH), dtype=jnp.float32) * scale
        wv = jax.random.normal(ks[3], (NH, DM, DH), dtype=jnp.float32) * scale
        wo = jax.random.normal(ks[4], (NH * DH, DM), dtype=jnp.float32) * (1.0 / (NH * DH)) ** 0.5
        return {'x': x, 'wq': wq, 'wk': wk, 'wv': wv, 'wo': wo}
    _L0_attn_in = _L0_attn_setup()

    def _L0_ffn_setup():
        import jax, jax.numpy as jnp
        import numpy as np
        HIDDEN = 512
        INTER = 2048
        key = jax.random.key(seed)
        k1, k2, k3, k4, k5 = jax.random.split(key, 5)
        hidden_states = jax.random.normal(k1, (4, 1024, HIDDEN), dtype=jnp.float32)
        W1 = jax.random.normal(k2, (HIDDEN, INTER), dtype=jnp.float32) * (1.0 / np.sqrt(HIDDEN))
        b1 = jax.random.normal(k3, (INTER,), dtype=jnp.float32) * 0.02
        W2 = jax.random.normal(k4, (INTER, HIDDEN), dtype=jnp.float32) * (1.0 / np.sqrt(INTER))
        b2 = jax.random.normal(k5, (HIDDEN,), dtype=jnp.float32) * 0.02
        return {'hidden_states': hidden_states, 'W1': W1, 'b1': b1, 'W2': W2, 'b2': b2}
    _L0_ffn_in = _L0_ffn_setup()
    _L0_c = _w((lambda *s: np.random.randn(*s).astype(np.float32) * 0.05)(8, 512))
    _L0_wmod = _w((lambda *s: np.random.randn(*s).astype(np.float32) * 0.05)(512, 6 * 512) * 512 ** (-0.5))
    _d = {'L0_attn_x': _L0_attn_in['x'], 'L0_attn_wq': _L0_attn_in['wq'], 'L0_attn_wk': _L0_attn_in['wk'], 'L0_attn_wv': _L0_attn_in['wv'], 'L0_attn_wo': _L0_attn_in['wo'], 'L0_ffn_W1': _L0_ffn_in['W1'], 'L0_ffn_b1': _L0_ffn_in['b1'], 'L0_ffn_W2': _L0_ffn_in['W2'], 'L0_ffn_b2': _L0_ffn_in['b2'], 'L0_c': _L0_c, 'L0_wmod': _L0_wmod}
    _x0 = _d['L0_attn_x']
    _d['L0_attn_x'] = jax.random.normal(jax.random.fold_in(jax.random.key(seed), 1), (8, 1024, 512), dtype=_x0.dtype)
    del _x0
    return _d

def reference(L0_attn_x, L0_attn_wq, L0_attn_wk, L0_attn_wv, L0_attn_wo, L0_ffn_W1, L0_ffn_b1, L0_ffn_W2, L0_ffn_b2, L0_c, L0_wmod):

    def _L0_attn_ref(x, wq, wk, wv, wo):
        import jax, jax.numpy as jnp
        import numpy as np
        B, T, DM = (2, 1024, 512)
        DH = 128
        NH = DM // DH
        ROTARY_BASE = 10000.0

        def fractional_rope(x, base):
            dh = x.shape[-1]
            rot, skip = jnp.split(x, 2, axis=-1)
            width = rot.shape[-1]
            half = width // 2
            t = rot.shape[-2]
            positions = jnp.arange(t)[:, None]
            dims = jnp.arange(half)
            ang_freqs = jnp.power(base, -dims / half)[None, :]
            radians = positions * ang_freqs
            cos = jnp.cos(radians).astype(x.dtype)
            sin = jnp.sin(radians).astype(x.dtype)
            even, odd = jnp.split(rot, 2, axis=-1)
            r_even = even * cos - odd * sin
            r_odd = even * sin + odd * cos
            return jnp.concatenate([r_even, r_odd, skip], axis=-1)
        b, t, dm = x.shape
        q = jnp.einsum('btd,hdk->bhtk', x, wq)
        k = jnp.einsum('btd,hdk->bhtk', x, wk)
        v = jnp.einsum('btd,hdk->bhtk', x, wv)
        q = fractional_rope(q, ROTARY_BASE)
        k = fractional_rope(k, ROTARY_BASE)
        inv_sqrt_dh = DH ** (-0.5)
        q = q * inv_sqrt_dh
        k = k * inv_sqrt_dh
        s = jnp.einsum('bhik,bhjk->bhij', q, k)
        i = jnp.arange(t)[:, None]
        j = jnp.arange(t)[None, :]
        mask = jnp.less(i, j).astype(s.dtype)
        s = s - 1e+30 * mask
        p = jax.nn.softmax(s, axis=-1)
        o = jnp.einsum('bhij,bhjv->bihv', p, v)
        o = jnp.reshape(o, (b, t, NH * DH))
        return jnp.einsum('bto,od->btd', o, wo)

    def _L0_ffn_ref(hidden_states, W1, b1, W2, b2):
        import jax, jax.numpy as jnp
        import numpy as np
        HIDDEN = 512
        INTER = 2048
        h = jax.nn.relu(jnp.einsum('bsh,hi->bsi', hidden_states, W1) + b1)
        return jnp.einsum('bsi,ih->bsh', h, W2) + b2
    x = L0_attn_x
    mod = (_silu(L0_c) @ L0_wmod).reshape(L0_c.shape[0], 6, 1, -1)
    sa, ca, ga, sb, cb, gb = (mod[:, 0], mod[:, 1], mod[:, 2], mod[:, 3], mod[:, 4], mod[:, 5])
    ga = (2 * (ga >= 0) - 1) * jnp.maximum(jnp.abs(ga), 0.25)
    gb = (2 * (gb >= 0) - 1) * jnp.maximum(jnp.abs(gb), 0.25)
    h = _layernorm(x, axis=-1) * (1 + ca) + sa
    x = x + ga * _L0_attn_ref(h, L0_attn_wq, L0_attn_wk, L0_attn_wv, L0_attn_wo)
    h = _layernorm(x, axis=-1) * (1 + cb) + sb
    x = x + gb * _L0_ffn_ref(h, L0_ffn_W1, L0_ffn_b1, L0_ffn_W2, L0_ffn_b2)
    return x

_drawn_inputs = setup_inputs


def setup_inputs(seed=0):
    import zlib

    import numpy as np

    out = dict(_drawn_inputs(seed))
    spreads = {}
    factors = {'L0_attn_wq': 8.0, 'L0_attn_wk': 8.0, 'L0_ffn_b1': 8.0, 'L0_ffn_b2': 8.0}
    for name, (base, spread) in spreads.items():
        noise = np.random.default_rng([zlib.crc32(name.encode()), seed]).standard_normal(out[name].shape)
        drawn = base * np.exp(spread * noise) if base else spread * noise
        out[name] = jnp.asarray(drawn.astype(out[name].dtype))
    for name, factor in factors.items():
        out[name] = (out[name] * factor).astype(out[name].dtype)
    return out
```

```python
from contextlib import ExitStack

import numpy as np

import concourse.bass as bass
from concourse import mybir

F32 = mybir.dt.float32
F32R = mybir.dt.float32r
BF16 = mybir.dt.bfloat16
ALU = mybir.AluOpType
ACT = mybir.ActivationFunctionType
AX = mybir.AxisListType

P = 128
B, T, D = 8, 1024, 512
H, DH = 4, 128
INTER = 2048
KB = D // P
NT = T // P
IB = INTER // P
ROT = DH // 2
HALF = ROT // 2
QKV = 3 * DH
EPS = 1e-5
GATE_MIN = 0.25
MASKED = -1e30
STEPS = H * NT
CHUNKS = NT + NT // 2
GT = 4
GROUPS = NT // GT
SA, CA, GA, SB, CB, GB, B2G = range(7)
WO_STEP = [2, 3, 4, 6, 7, 8, 10, 11]
LN_STEP = (H - 2) * NT
LN_EVERY = 2
TAIL_STEPS = 14


def p_column(i):
    return P * (i * (i + 1) // 2)


def chunks_of(i):
    return [2 * i, 2 * i + 1] if i < NT // 2 else [NT // 2 + i]


class Step:

    def __init__(self, b, k, kind):
        self.b, self.k, self.kind = b, k, kind
        self.h, self.i = divmod(k, NT)
        self.n = b * STEPS + k
        self.scores = kind != "tail"
        self.project = self.has_project(k)
        self.turn = k == 0 and kind != "tail" or k > 0 and self.has_project(k - 1)
        self.out = [j for j, s in enumerate(WO_STEP) if s == k] if kind != "first" else []

    def has_project(self, k):
        return self.kind in ("first", "middle") or (self.kind == "last" and k < STEPS - NT)

    def has_chunk(self, s):
        if s < NT:
            return not (self.kind == "first" and self.h == 0 or self.kind == "tail" and self.h > 0)
        return self.kind != "tail"

    def chunk_count(self, s):
        return self.b * (H * CHUNKS) + self.h * CHUNKS + s + 1 - NT

    def chunk(self, s):
        if s < 0:
            return 0, GT - 1, (self.h + 1) % 2
        if s < NT:
            return 1, s, (self.h + 1) % 2
        return 0, s - NT, self.h % 2

    def ln(self, step):
        t, rest = divmod(self.k - LN_STEP - step, LN_EVERY)
        return t if self.kind in ("first", "middle") and rest == 0 and 0 <= t < NT else None


def batch_rows(engine, body):
    body(0, "first", STEPS)
    with engine.Fori(1, B - 1) as b:
        body(b, "middle", STEPS)
    body(B - 1, "last", STEPS)
    body(B, "tail", TAIL_STEPS)


def wait_alone(engine, semaphore, value, passed, at_least):
    value = value if isinstance(value, int) else engine.to_reg(value)
    engine.wait_ge(passed, at_least)
    engine.wait_ge(semaphore, value)


def prepare(nc, t, mod_table, w):
    with ExitStack() as ctx:
        def sb(name, shape, dt=F32):
            return ctx.enter_context(nc.sbuf_tensor(name, shape, dt))

        def sem(name):
            return ctx.enter_context(nc.semaphore(name))

        stage = sb("weight_stage", [P, 2, 4, H, DH])
        wmod = sb("wmod_stage", [P, KB, 6 * D])
        mask = sb("mask", [P, P])
        c_cols = sb("c_cols", [P, KB, B])
        e_cols = sb("e_cols", [P, KB, B])
        d_cols = sb("d_cols", [P, KB, B])
        r_cols = sb("r_cols", [P, KB, B])
        silu = sb("silu", [P, KB, B])
        rows = sb("mod_rows", [B, 7, D])
        b2_rows = sb("b2_rows", [B, D])
        mag = sb("gate_magnitude", [B, 2, D])
        sign = sb("gate_sign", [B, 2, D])
        acc = [ctx.enter_context(nc.psum_tensor(f"mod_acc{r}", [P, D], F32)) for r in range(6)]

        c_in = sem("c_loaded")
        const_in = sem("tables_loaded")
        wmod_in = [sem(f"wmod{k}_loaded") for k in range(KB)]
        stage_in = [sem(f"stage{j}_loaded") for j in range(2)]
        split = sem("weights_split")
        exp_done = sem("exp_done")
        chain = sem("vector_chain")
        silu_done = sem("silu_done")
        acc_done = sem("mod_rows_multiplied")
        rows_done = sem("mod_rows_done")
        stored = sem("mod_rows_stored")
        sources = [t["wq"], t["wk"], t["wv"]]

        block = ctx.enter_context(nc.Block())

        @block.sync
        def _(sp):
            for kb in range(KB):
                sp.dma_start(c_cols[:, kb, :], t["c"][:, kb * P:(kb + 1) * P].rearrange("b p -> p b"),
                             allow_slow_non_contiguous=True).then_inc(c_in, 16)
            sp.dma_start(w["cos"][:], t["cos"]).then_inc(const_in, 16)
            sp.dma_start(w["sin"][:], t["sin"]).then_inc(const_in, 16)
            sp.dma_start(w["ident"][:], t["ident"]).then_inc(const_in, 16)
            sp.dma_start(mask[:], t["mask"]).then_inc(const_in, 16)
            sp.dma_start(b2_rows[:], t["b2"].rearrange("(a d) -> a d", a=1).to_broadcast([B, D])).then_inc(const_in, 16)
            for k in range(KB):
                sp.dma_start(wmod[:, k, :], t["wmod"][k * P:(k + 1) * P, :]).then_inc(wmod_in[k], 16)
            sp.wait_ge(rows_done, 1)
            sp.dma_start(mod_table, rows[:]).then_inc(stored, 16)
            sp.wait_ge(stored, 16)

        @block.scalar
        def _(act):
            for j in range(4):
                if j >= 2:
                    act.wait_ge(split, 2 * (j - 1))
                for kb in range(KB):
                    if j < 3:
                        src = sources[j][:, kb * P:(kb + 1) * P, :].rearrange("h p k -> p h k")
                        act.dma_start(stage[:, j % 2, kb, :, :], src).then_inc(stage_in[j % 2], 16)
                    else:
                        act.dma_start(stage[:, 1, kb, :, :].rearrange("p h k -> p (h k)"),
                                      t["wo"][kb * P:(kb + 1) * P, :]).then_inc(stage_in[1], 16)
                if j == 1:
                    act.wait_ge(c_in, 16 * KB)
                    act.activation(e_cols[:], c_cols[:], ACT.Exp, scale=-1.0).then_inc(exp_done, 1)

        @block.vector
        def _(dve):
            n = [0]

            def link(ins):
                n[0] += 1
                ins.then_inc(chain, 1)
                dve.wait_ge(chain, n[0])

            def weights(j):
                dve.wait_ge(stage_in[j % 2], 16 * KB * (j // 2 + 1))
                for kb in range(KB):
                    src = stage[:, j % 2, kb, :, :]
                    if j < 3:
                        hi = w["wqkv_hi"][:, kb, :, j * DH:(j + 1) * DH]
                        lo = w["wqkv_lo"][:, kb, :, j * DH:(j + 1) * DH]
                    else:
                        hi = w["wo_hi"][:, kb, :].rearrange("p (h k) -> p h k", h=H)
                        lo = w["wo_lo"][:, kb, :].rearrange("p (h k) -> p h k", h=H)
                    f = 1.0 / DH if j == 0 else 1.0
                    if f == 1.0:
                        link(dve.tensor_copy(hi, src))
                    else:
                        link(dve.tensor_scalar(hi, src, f, None, ALU.mult))
                    ins = dve.scalar_tensor_tensor(out=lo, in0=src, scalar=f, in1=hi.bitcast(F32),
                                                   op0=ALU.mult, op1=ALU.subtract)
                ins.then_inc(split, 2)

            dve.wait_ge(const_in, 16 * 5)
            dve.tensor_copy(w["ident16"][:], w["ident"][:])
            dve.tensor_copy(w["mask16"][:], mask[:])
            dve.wait_ge(exp_done, 1)
            link(dve.tensor_scalar(d_cols[:], e_cols[:], 1.0, None, ALU.add))
            link(dve.reciprocal(r_cols[:], d_cols[:]))
            dve.tensor_tensor(silu[:], c_cols[:], r_cols[:], ALU.mult).then_inc(silu_done, 1)
            for j in range(4):
                weights(j)
            dve.wait_ge(acc_done, 1)
            for r in (SA, SB):
                dve.tensor_copy(rows[:, r, :], acc[r][0:B, :])
            for r in (CA, CB):
                dve.tensor_scalar(rows[:, r, :], acc[r][0:B, :], 1.0, None, ALU.add)
            for j, r in enumerate((GA, GB)):
                dve.tensor_scalar(mag[:, j, :], acc[r][0:B, :], -1.0, None, ALU.mult)
                link(dve.tensor_scalar(sign[:, j, :], acc[r][0:B, :], 0.0, 2.0, ALU.is_ge, ALU.mult))
                link(dve.tensor_tensor(mag[:, j, :], acc[r][0:B, :], mag[:, j, :], ALU.max))
                link(dve.tensor_scalar(mag[:, j, :], mag[:, j, :], GATE_MIN, None, ALU.max))
                link(dve.scalar_tensor_tensor(out=rows[:, r, :], in0=sign[:, j, :], scalar=-1.0,
                                              in1=mag[:, j, :], op0=ALU.add, op1=ALU.mult))
            dve.tensor_tensor(rows[:, B2G, :], rows[:, GB, :], b2_rows[:], ALU.mult).then_inc(rows_done, 1)

        @block.tensor
        def _(pe):
            pe.wait_ge(silu_done, 1)
            for k in range(KB):
                pe.wait_ge(wmod_in[k], 16)
                for r in range(6):
                    ins = pe.matmul(acc[r][0:B, :], silu[:, k, :], wmod[:, k, r * D:(r + 1) * D],
                                    start=(k == 0), stop=(k == KB - 1))
            ins.then_inc(acc_done, 1)


def attention(nc, t, mod_table, x1, w):
    x_tiles = t["x"].rearrange("b (i p) d -> b i p d", p=P)
    x1_tiles = x1.rearrange("b (i p) d -> b i p d", p=P)

    with ExitStack() as ctx:
        def sb(name, shape, dt=F32):
            return ctx.enter_context(nc.sbuf_tensor(name, shape, dt))

        def psum(name, shape):
            return ctx.enter_context(nc.psum_tensor(name, shape, F32))

        def sem(name):
            return ctx.enter_context(nc.semaphore(name))

        def pair(name, shape):
            return sb(name + "_hi", shape, F32R), sb(name + "_lo", shape, F32R)

        wqkv_hi, wqkv_lo, wo_hi, wo_lo = w["wqkv_hi"], w["wqkv_lo"], w["wo_hi"], w["wo_lo"]
        ident = w["ident"]
        hT_hi, hT_lo = pair("hT", [P, KB, T])
        qT_hi, qT_lo = pair("qT", [P, T])
        kT_hi, kT_lo = pair("kT", [P, 2, T])
        v_hi, v_lo = pair("v", [P, 2, NT, DH])
        pT_hi, pT_lo = pair("pT", [P, 2, GT * P])
        oT_tile_hi, oT_tile_lo = pair("oT_tile", [P, H, P])
        probs = sb("probs", [P, p_column(NT)])
        oT = sb("oT", [P, H, T])
        x_ln = sb("x_ln", [P, 2, D])
        x_res = sb("x_res", [P, 2, D])
        gated = sb("gated", [P, D])
        nat = sb("qkv_natural", [P, 2, QKV])
        by_cos = sb("by_cos", [P, 2, ROT])
        by_sin = sb("by_sin", [P, 2, ROT])
        row_ca = sb("row_ca", [P, D])
        row_sa = sb("row_sa", [P, D])
        row_ga = sb("row_ga", [P, D])
        stats = sb("stats", [P, 2, 6])
        mean_var = sb("mean_var", [P, 2, 2])
        rstd = sb("rstd", [P, 2, 1])
        minus_half = sb("minus_half", [P, 1])
        neg_max = sb("neg_max", [P, NT])
        row_sum = sb("row_sum", [P, NT])
        inv_sum = sb("inv_sum", [P, NT])

        s_ps = psum("scores_ps", [P, T])
        qkv_ps = psum("qkv_ps", [P, 512])
        turn_ps = psum("turn_ps", [P, 512])
        pT_ps = [psum(f"pT_ps{j}", [P, GT * P]) for j in range(2)]
        o_ps = psum("o_ps", [P, GT * P])
        mix_ps = psum("mix_ps", [P, D])

        scores_done = sem("scores_done")
        qkv_done = sem("qkv_done")
        turned = sem("qk_turned")
        pT_done = sem("pT_done")
        pv_done = sem("pv_done")
        ln_turned = sem("ln_turned")
        y_done = sem("y_done")
        nat_copied = sem("nat_copied")
        exp_done = sem("exp_done")
        qk_hi_done = sem("qk_hi_done")
        pT_hi_done = sem("pT_hi_done")
        oT_done = sem("oT_done")
        hT_hi_done = sem("hT_hi_done")
        ropes_done = sem("ropes_done")
        v_lo_done = sem("v_lo_done")
        max_done = sem("max_done")
        inv_done = sem("inv_done")
        qk_lo_done = sem("qk_lo_done")
        pT_lo_done = sem("pT_lo_done")
        hT_lo_done = sem("hT_lo_done")
        bn_done = sem("bn_done")
        mv_done = sem("mean_var_done")
        scaled = sem("x_scaled")
        normed = sem("x_normed")
        gated_done = sem("gated_done")
        half_set = sem("minus_half_set")
        rotated = sem("rotated")
        v_hi_done = sem("v_hi_done")
        probs_done = sem("probs_normalised")
        last_probs_done = sem("last_probs_normalised")
        eps_done = sem("eps_added")
        rstd_done = sem("rstd_done")
        oT_hi_done = sem("oT_tile_hi_done")
        oT_lo_done = sem("oT_tile_lo_done")
        x1_done = sem("x1_done")
        x_ln_in = [sem(f"x_ln{j}_loaded") for j in range(2)]
        x_res_in = [sem(f"x_res{j}_loaded") for j in range(2)]
        x1_out = [sem(f"x1_{j}_stored") for j in range(2)]
        ln_rows_in = sem("ln_rows_loaded")
        ga_in = sem("ga_loaded")

        block = ctx.enter_context(nc.Block())

        @block.sync
        def _(sp):
            def load_ln(b, i):
                if not (isinstance(b, int) and b == 0 and i < 2):
                    sp.wait_ge(ln_turned, b * NT + i - 1)
                sp.dma_start(x_ln[:, i % 2, :], x_tiles[b, i]).then_inc(x_ln_in[i % 2], 16)

            def load_ln_rows(b):
                if not (isinstance(b, int) and b == 0):
                    sp.wait_ge(normed, b * NT)
                sp.dma_start(row_ca[:], mod_table[b, CA, :].partition_broadcast(P)).then_inc(ln_rows_in, 16)
                sp.dma_start(row_sa[:], mod_table[b, SA, :].partition_broadcast(P)).then_inc(ln_rows_in, 16)

            def load_ga(b):
                if not (isinstance(b, int) and b == 0):
                    sp.wait_ge(gated_done, b * NT)
                sp.dma_start(row_ga[:], mod_table[b, GA, :].partition_broadcast(P)).then_inc(ga_in, 16)

            def load_res(b, i):
                if not (isinstance(b, int) and b == 0 and i < 2):
                    sp.wait_ge(x1_out[i % 2], b * (NT // 2 * 16) + i // 2 * 16)
                sp.dma_start(x_res[:, i % 2, :], x_tiles[b, i]).then_inc(x_res_in[i % 2], 16)

            def store(b, i):
                wait_alone(sp, x1_done, b * NT + i + 1, ga_in, 16)
                sp.dma_start(x1_tiles[b, i], x_res[:, i % 2, :]).then_inc(x1_out[i % 2], 16)

            load_ln_rows(0)
            for i in range(NT):
                load_ln(0, i)

            def body(b, kind, steps):
                for k in range(steps):
                    st = Step(b, k, kind)
                    if k == 1 and kind in ("first", "middle"):
                        load_ln_rows(b + 1)
                    for j in [j for j, s in enumerate(WO_STEP) if kind != "first" and s + 1 == k]:
                        store(b - 1, j)
                        if j + 2 < NT:
                            load_res(b - 1, j + 2)
                    if k == WO_STEP[-1] + 2 and kind != "tail":
                        load_ga(b)
                        load_res(b, 0)
                        load_res(b, 1)
                    t_ln = st.ln(-3)
                    if t_ln is not None:
                        load_ln(b + 1, t_ln)

            batch_rows(sp, body)
            for j in range(2):
                sp.wait_ge(x1_out[j], 16 * B * NT // 2)

        @block.tensor
        def _(pe):
            def three(out, a_hi, a_lo, b_hi, b_lo, start, stop):
                pe.matmul(out, a_hi, b_hi, start=start, stop=False)
                pe.matmul(out, a_hi, b_lo, start=False, stop=False)
                return pe.matmul(out, a_lo, b_hi, start=False, stop=stop)

            def project(b, h, i, kbs):
                if kbs[0] == 0:
                    pe.wait_ge(hT_lo_done, b * NT + i + 1)
                    if not (isinstance(b, int) and b == 0 and h == 0 and i == 0):
                        pe.wait_ge(nat_copied, b * STEPS + h * NT + i)
                cols = slice(i * P, (i + 1) * P)
                for kb in kbs:
                    ins = three(qkv_ps[:, 0:QKV], hT_hi[:, kb, cols], hT_lo[:, kb, cols],
                                wqkv_hi[:, kb, h, :], wqkv_lo[:, kb, h, :], kb == 0, kb == KB - 1)
                if kbs[-1] == KB - 1:
                    ins.then_inc(qkv_done, 1)

            def turn(n, i):
                pe.wait_ge(rotated, n + 1)
                if not (isinstance(n, int) and n == 0):
                    pe.wait_ge(qk_lo_done, n)
                pe.transpose(turn_ps[:, 0:P], nat[:, i % 2, 0:DH], ident[:])
                pe.transpose(turn_ps[:, P:2 * P], nat[:, i % 2, DH:2 * DH], ident[:]).then_inc(turned, 1)

            def scores(st):
                i, par = st.i, st.h % 2
                pe.wait_ge(qk_lo_done, st.n + 1)
                if not (st.kind == "first" and st.k == 0):
                    pe.wait_ge(exp_done, st.n)
                q_cols = slice(i * P, (i + 1) * P)
                for c in range(0, (i + 1) * P, 512):
                    end = min((i + 1) * P, c + 512)
                    diagonal = end == (i + 1) * P
                    ins = three(s_ps[:, c:end], qT_hi[:, q_cols], qT_lo[:, q_cols],
                                kT_hi[:, par, c:end], kT_lo[:, par, c:end], True, not diagonal)
                    if diagonal:
                        ins = pe.matmul(s_ps[:, i * P:end], w["ident16"][:], w["mask16"][:],
                                        start=False, stop=True)
                ins.then_inc(scores_done, 1)

            def slot(st, s):
                if s < CHUNKS and st.has_chunk(s):
                    group, j, _ = st.chunk(s)
                    done = (st.b * H + st.h - (1 if group == 1 else 0)) * GROUPS + group + 1
                    pe.wait_ge(probs_done, done * (GT - 1))
                    pe.wait_ge(last_probs_done, done)
                    count = st.chunk_count(s)
                    if not (st.kind == "first" and st.h == 0 and s < NT + 2):
                        pe.wait_ge(pT_lo_done, count - 2)
                    for i in range(max(j, GT * group), GT * group + GT):
                        c = p_column(i) + j * P
                        o = (i - GT * group) * P
                        ins = pe.transpose(pT_ps[s % 2][:, o:o + P], probs[:, c:c + P], ident[:])
                    ins.then_inc(pT_done, 1)
                if st.has_chunk(s - 1):
                    group, j, par = st.chunk(s - 1)
                    pe.wait_ge(pT_lo_done, st.chunk_count(s - 1))
                    if j == 0 and not (st.kind == "first" and st.h == 0):
                        before = st.b * (2 * H) + 2 * st.h + (0 if group == 0 else -1)
                        pe.wait_ge(oT_done, before)
                    c0 = max(0, j - GT * group) * P
                    buf = (s - 1) % 2
                    three(o_ps[:, c0:], v_hi[:, par, j, :], v_lo[:, par, j, :],
                          pT_hi[:, buf, c0:], pT_lo[:, buf, c0:], j == 0,
                          j == GT * group + GT - 1).then_inc(pv_done, 1)

            def turn_ln(b, i):
                pe.wait_ge(normed, b * NT + i + 1)
                if not (isinstance(b, int) and b == 0 and i == 0):
                    pe.wait_ge(hT_lo_done, b * NT + i)
                if i == 0 and not (isinstance(b, int) and b <= 1):
                    pe.wait_ge(gated_done, (b - 1) * NT)
                for kb in range(KB):
                    ins = pe.transpose(mix_ps[:, kb * P:(kb + 1) * P], x_ln[:, i % 2, kb * P:(kb + 1) * P], ident[:])
                ins.then_inc(ln_turned, 1)

            def output(b, i):
                pe.wait_ge(oT_lo_done, b * NT + i + 1)
                if i == 0:
                    if not (isinstance(b, int) and b == B - 1):
                        pe.wait_ge(hT_lo_done, (b + 2) * NT)
                else:
                    pe.wait_ge(gated_done, b * NT + i)
                for h in range(H):
                    ins = three(mix_ps[:], oT_tile_hi[:, h, :], oT_tile_lo[:, h, :],
                                wo_hi[:, h, :], wo_lo[:, h, :], h == 0, h == H - 1)
                ins.then_inc(y_done, 1)

            for i in range(NT):
                turn_ln(0, i)
                if i > 0:
                    project(0, 0, i - 1, range(KB))
                if i > 1:
                    turn(i - 2, i - 2)
            project(0, 0, NT - 1, range(KB))
            turn(NT - 2, NT - 2)

            def body(b, kind, steps):
                for k in range(steps):
                    st = Step(b, k, kind)
                    i = st.i
                    nb, nh = (b + 1, 0) if st.h == H - 1 else (b, st.h + 1)
                    if kind == "tail" and k >= NT:
                        for j in st.out:
                            output(b - 1, j)
                        continue
                    if st.scores:
                        scores(st)
                    todo = chunks_of(i)
                    slot(st, todo[0])
                    if st.project:
                        project(nb, nh, i, range(0, KB // 2))
                    if len(todo) > 1:
                        slot(st, todo[1])
                    if st.project:
                        project(nb, nh, i, range(KB // 2, KB))
                    if st.turn:
                        turn(st.n + NT - 1, (i - 1) % NT)
                    for j in st.out:
                        output(b - 1, j)
                    t_ln = st.ln(0)
                    if t_ln is not None:
                        turn_ln(b + 1, t_ln)

            batch_rows(pe, body)

        @block.scalar
        def _(act):
            def natural(n, i):
                act.wait_ge(qkv_done, n + 1)
                if not (isinstance(n, int) and n < 2):
                    act.wait_ge(turned, n - 1)
                    act.wait_ge(v_lo_done, n - 1)
                act.activation(nat[:, i % 2, :], qkv_ps[:, 0:QKV], ACT.Copy).then_inc(nat_copied, 1)

            def v_high(n, i, par):
                act.wait_ge(nat_copied, n + 1)
                act.activation(v_hi[:, par, i, :], nat[:, i % 2, 2 * DH:QKV], ACT.Copy).then_inc(v_hi_done, 1)

            def oT_tile_hi_of(b, i):
                act.wait_ge(oT_done, b * (2 * H) + 2 * H - 1 + i // GT)
                if not (isinstance(b, int) and b == 0 and i == 0):
                    act.wait_ge(y_done, b * NT + i)
                act.activation(oT_tile_hi[:], oT[:, :, i * P:(i + 1) * P], ACT.Copy).then_inc(oT_hi_done, 1)

            def qk_hi(n, i, par):
                act.wait_ge(turned, n + 1)
                cols = slice(i * P, (i + 1) * P)
                act.activation(qT_hi[:, cols], turn_ps[:, 0:P], ACT.Copy)
                act.activation(kT_hi[:, par, cols], turn_ps[:, P:2 * P], ACT.Copy).then_inc(qk_hi_done, 1)

            def hT_hi_of(b, i):
                act.wait_ge(ln_turned, b * NT + i + 1)
                act.activation(hT_hi[:, :, i * P:(i + 1) * P], mix_ps[:].rearrange("p (k c) -> p k c", k=KB),
                               ACT.Copy).then_inc(hT_hi_done, 1)

            def pT_hi_of(st, s):
                if s < CHUNKS and st.has_chunk(s):
                    group, j, _ = st.chunk(s)
                    c0 = max(0, j - GT * group) * P
                    act.wait_ge(pT_done, st.chunk_count(s))
                    act.activation(pT_hi[:, s % 2, c0:], pT_ps[s % 2][:, c0:], ACT.Copy).then_inc(pT_hi_done, 1)

            def attended(st, s):
                if st.has_chunk(s - 1):
                    group, _, _ = st.chunk(s - 1)
                    act.wait_ge(pv_done, st.chunk_count(s - 1))
                    head = (st.h - 1) % H
                    if head == 0 and not (st.kind == "first"):
                        act.wait_ge(oT_lo_done, (st.b - 1) * NT + (group + 1) * GT)
                    act.activation(oT[:, head, group * GT * P:(group + 1) * GT * P], o_ps[:],
                                   ACT.Copy).then_inc(oT_done, 1)

            def exps(st):
                i = st.i
                W = (i + 1) * P
                act.wait_ge(max_done, st.n + 1)
                act.activation(probs[:, p_column(i):p_column(i) + W], s_ps[:, 0:W], ACT.Exp,
                               bias=neg_max[:, i:i + 1], accum_out=row_sum[:, i:i + 1]).then_inc(exp_done, 1)

            for i in range(NT):
                hT_hi_of(0, i)
                if i > 0:
                    natural(i - 1, i - 1)
                    v_high(i - 1, i - 1, 0)
                if i > 1:
                    qk_hi(i - 2, i - 2, 0)
            natural(NT - 1, NT - 1)
            v_high(NT - 1, NT - 1, 0)
            qk_hi(NT - 2, NT - 2, 0)

            def body(b, kind, steps):
                for k in range(steps):
                    st = Step(b, k, kind)
                    i = st.i
                    todo = chunks_of(i)
                    if st.turn and (k > 0 or kind != "first"):
                        natural(st.n + NT - 1, (i - 1) % NT)
                    if kind == "tail" and k > NT // 2:
                        for j in st.out:
                            oT_tile_hi_of(b - 1, j)
                        continue
                    if i == 0:
                        attended(st, 0)
                    if len(todo) > 1:
                        pT_hi_of(st, todo[0])
                    if st.turn and (k > 0 or kind != "first"):
                        v_high(st.n + NT - 1, (i - 1) % NT, (st.h + (i > 0)) % 2)
                    for j in st.out:
                        oT_tile_hi_of(b - 1, j)
                    if st.scores:
                        exps(st)
                    if i == NT // 2:
                        attended(st, NT)
                    pT_hi_of(st, todo[-1])
                    if st.turn:
                        qk_hi(st.n + NT - 1, (i - 1) % NT, (st.h + (i > 0)) % 2)
                    t_ln = st.ln(0)
                    if t_ln is not None:
                        hT_hi_of(b + 1, t_ln)

            batch_rows(act, body)

        @block.vector
        def _(dve):
            def ropes(n, i):
                dve.wait_ge(nat_copied, n + 1)
                if not (isinstance(n, int) and n == 0):
                    dve.wait_ge(rotated, n)
                qk = nat[:, i % 2, 0:2 * DH].rearrange("p (t c) -> p t c", t=2)
                even, odd = slice(0, HALF), slice(HALF, ROT)

                def table(name, part):
                    return w[name][:, i:i + 1, part].to_broadcast([P, 2, part.stop - part.start])

                dve.tensor_tensor(by_cos[:], qk[:, :, 0:ROT], table("cos", slice(0, ROT)), ALU.mult)
                dve.tensor_tensor(by_sin[:, :, even], qk[:, :, odd], table("sin", even), ALU.mult)
                dve.tensor_tensor(by_sin[:, :, odd], qk[:, :, even], table("sin", odd), ALU.mult).then_inc(ropes_done, 1)

            def rotate(n, i):
                dve.wait_ge(ropes_done, n + 1)
                qk = nat[:, i % 2, 0:2 * DH].rearrange("p (t c) -> p t c", t=2)
                dve.tensor_tensor(qk[:, :, 0:ROT], by_cos[:], by_sin[:], ALU.add).then_inc(rotated, 1)

            def v_low(n, i, par):
                dve.wait_ge(v_hi_done, n + 1)
                dve.tensor_tensor(v_lo[:, par, i, :], nat[:, i % 2, 2 * DH:QKV], v_hi[:, par, i, :].bitcast(F32),
                                  ALU.subtract).then_inc(v_lo_done, 1)

            def qk_lo(n, i, par):
                dve.wait_ge(qk_hi_done, n + 1)
                cols = slice(i * P, (i + 1) * P)
                dve.tensor_tensor(qT_lo[:, cols], turn_ps[:, 0:P], qT_hi[:, cols].bitcast(F32), ALU.subtract)
                dve.tensor_tensor(kT_lo[:, par, cols], turn_ps[:, P:2 * P], kT_hi[:, par, cols].bitcast(F32),
                                  ALU.subtract).then_inc(qk_lo_done, 1)

            def hT_lo_of(b, i):
                dve.wait_ge(hT_hi_done, b * NT + i + 1)
                dve.tensor_tensor(hT_lo[:, :, i * P:(i + 1) * P], mix_ps[:].rearrange("p (k c) -> p k c", k=KB),
                                  hT_hi[:, :, i * P:(i + 1) * P].bitcast(F32), ALU.subtract).then_inc(hT_lo_done, 1)

            def pT_lo_of(st, s):
                if s < CHUNKS and st.has_chunk(s):
                    group, j, _ = st.chunk(s)
                    c0 = max(0, j - GT * group) * P
                    dve.wait_ge(pT_hi_done, st.chunk_count(s))
                    dve.tensor_tensor(pT_lo[:, s % 2, c0:], pT_ps[s % 2][:, c0:], pT_hi[:, s % 2, c0:].bitcast(F32),
                                      ALU.subtract).then_inc(pT_lo_done, 1)

            def maxima(st):
                i = st.i
                dve.wait_ge(scores_done, st.n + 1)
                dve.tensor_reduce(neg_max[:, i:i + 1], s_ps[:, 0:(i + 1) * P], AX.X, ALU.max,
                                  negate=True).then_inc(max_done, 1)

            def inverse(st):
                dve.wait_ge(exp_done, st.n + 1)
                dve.reciprocal(inv_sum[:, st.i:st.i + 1], row_sum[:, st.i:st.i + 1]).then_inc(inv_done, 1)

            def normalise(st):
                i = st.i
                dve.wait_ge(inv_done, st.n + 1)
                p = probs[:, p_column(i):p_column(i + 1)]
                dve.tensor_scalar(p, p, inv_sum[:, i:i + 1], None, ALU.mult).then_inc(last_probs_done, 1)

            def ln_stats(b, i):
                dve.wait_ge(x_ln_in[i % 2], b * (NT // 2 * 16) + (i // 2 + 1) * 16)
                dve.bn_stats(stats[:, i % 2, :], x_ln[:, i % 2, :]).then_inc(bn_done, 1)
                wait_alone(dve, bn_done, b * NT + i + 1, bn_done, 1)
                dve.bn_aggr(mean_var[:, i % 2, :], stats[:, i % 2, :]).then_inc(mv_done, 1)

            def ln_apply(b, i):
                x = x_ln[:, i % 2, :]
                if i == 0:
                    dve.wait_ge(ln_rows_in, b * 32 + 32)
                dve.wait_ge(mv_done, b * NT + i + 1)
                dve.scalar_tensor_tensor(out=x, in0=x, scalar=mean_var[:, i % 2, 0:1], in1=row_ca[:],
                                         op0=ALU.subtract, op1=ALU.mult).then_inc(scaled, 1)
                dve.wait_ge(scaled, b * NT + i + 1)
                dve.wait_ge(rstd_done, b * NT + i + 1)
                dve.scalar_tensor_tensor(out=x, in0=x, scalar=rstd[:, i % 2, :], in1=row_sa[:],
                                         op0=ALU.mult, op1=ALU.add).then_inc(normed, 1)

            def oT_tile_lo_of(b, i):
                dve.wait_ge(oT_hi_done, b * NT + i + 1)
                dve.tensor_tensor(oT_tile_lo[:], oT[:, :, i * P:(i + 1) * P], oT_tile_hi[:].bitcast(F32),
                                  ALU.subtract).then_inc(oT_lo_done, 1)

            def gate(b, i):
                dve.wait_ge(y_done, b * NT + i + 1)
                if i == 0:
                    dve.wait_ge(ga_in, b * 16 + 16)
                if not (isinstance(b, int) and b == 0 and i == 0):
                    dve.wait_ge(x1_done, b * NT + i)
                dve.tensor_tensor(gated[:], mix_ps[:], row_ga[:], ALU.mult).then_inc(gated_done, 1)

            ln_stats(0, 0)
            for i in range(NT):
                ln_apply(0, i)
                if i + 1 < NT:
                    ln_stats(0, i + 1)
                hT_lo_of(0, i)
                if i > 0:
                    ropes(i - 1, i - 1)
                    v_low(i - 1, i - 1, 0)
                    rotate(i - 1, i - 1)
                if i > 1:
                    qk_lo(i - 2, i - 2, 0)
            ropes(NT - 1, NT - 1)
            v_low(NT - 1, NT - 1, 0)
            rotate(NT - 1, NT - 1)
            qk_lo(NT - 2, NT - 2, 0)

            def body(b, kind, steps):
                for k in range(steps):
                    st = Step(b, k, kind)
                    i = st.i
                    todo = chunks_of(i)
                    if st.scores:
                        maxima(st)
                    if len(todo) > 1:
                        pT_lo_of(st, todo[0])
                    if st.turn and (k > 0 or kind != "first"):
                        n = st.n + NT - 1
                        ropes(n, (i - 1) % NT)
                        v_low(n, (i - 1) % NT, (st.h + (i > 0)) % 2)
                        rotate(n, (i - 1) % NT)
                    for j in st.out:
                        oT_tile_lo_of(b - 1, j)
                    if st.scores:
                        inverse(st)
                        if i % GT == GT - 1:
                            normalise(st)
                    if kind != "first":
                        for j in [j for j, s in enumerate(WO_STEP) if s + 1 == k]:
                            gate(b - 1, j)
                    t_ln = st.ln(0)
                    if t_ln is not None:
                        ln_apply(b + 1, t_ln)
                    if kind == "tail" and k >= NT:
                        continue
                    pT_lo_of(st, todo[-1])
                    if st.turn:
                        qk_lo(st.n + NT - 1, (i - 1) % NT, (st.h + (i > 0)) % 2)
                    if t_ln is not None:
                        hT_lo_of(b + 1, t_ln)
                    t_ln = st.ln(-1)
                    if t_ln is not None:
                        ln_stats(b + 1, t_ln)

            batch_rows(dve, body)

        @block.gpsimd
        def _(pool):
            pool.memset(minus_half[:], -0.5).then_inc(half_set, 1)
            pool.wait_ge(half_set, 1)

            def normalise(st):
                i = st.i
                wait_alone(pool, inv_done, st.n + 1, half_set, 1)
                p = probs[:, p_column(i):p_column(i + 1)]
                pool.tensor_scalar(p, p, inv_sum[:, i:i + 1], None, ALU.mult).then_inc(probs_done, 1)

            def inverse_deviation(b, i):
                wait_alone(pool, mv_done, b * NT + i + 1, half_set, 1)
                pool.tensor_scalar(rstd[:, i % 2, :], mean_var[:, i % 2, 1:2], EPS, None, ALU.add).then_inc(eps_done, 1)
                pool.wait_ge(eps_done, b * NT + i + 1)
                pool.tensor_tensor(rstd[:, i % 2, :], rstd[:, i % 2, :], minus_half[:], ALU.pow).then_inc(rstd_done, 1)

            def residual(b, i):
                pool.wait_ge(gated_done, b * NT + i + 1)
                pool.wait_ge(x_res_in[i % 2], b * (NT // 2 * 16) + (i // 2 + 1) * 16)
                x = x_res[:, i % 2, :]
                pool.tensor_tensor(x, x, gated[:], ALU.add).then_inc(x1_done, 1)

            for i in range(NT):
                inverse_deviation(0, i)

            def body(b, kind, steps):
                for k in range(steps):
                    st = Step(b, k, kind)
                    i = st.i
                    if kind != "first":
                        for j in [j for j, s in enumerate(WO_STEP) if s + 1 == k]:
                            residual(b - 1, j)
                    if st.scores and i % GT < GT - 1:
                        normalise(st)
                    t_ln = st.ln(-1)
                    if t_ln is not None:
                        inverse_deviation(b + 1, t_ln)

            batch_rows(pool, body)


def ffn(nc, t, mod_table, x1, out):
    x1_groups = x1.rearrange("b (g i p) d -> b g p i d", p=P, i=GT)
    out_groups = out.rearrange("b (g i p) d -> b g p i d", p=P, i=GT)
    N = GT * P
    LN_SLOT = [4, 7, 10, 13]

    with ExitStack() as ctx:
        def sb(name, shape, dt=F32):
            return ctx.enter_context(nc.sbuf_tensor(name, shape, dt))

        def psum(name):
            return ctx.enter_context(nc.psum_tensor(name, [P, 512], F32))

        def sem(name):
            return ctx.enter_context(nc.semaphore(name))

        w1_hi = sb("w1_hi", [P, KB, INTER], F32R)
        w1_lo = sb("w1_lo", [P, KB, INTER], F32R)
        w2_hi = sb("w2_hi", [P, IB, D], F32R)
        w2_lo = sb("w2_lo", [P, IB, D], F32R)
        x = sb("x1_group", [P, 2, GT, D])
        xn = sb("x1_normed", [P, 2, D])
        hT_hi = sb("h2T_hi", [P, 2, KB, N], F32R)
        hT_lo = sb("h2T_lo", [P, 2, KB, N], F32R)
        relu = sb("relu", [P, 2, N])
        aT_hi = sb("aT_hi", [P, 2, N], F32R)
        aT_lo = sb("aT_lo", [P, 2, N], F32R)
        gated = sb("z_gated", [P, 2, D])
        row_cb = sb("row_cb", [P, D])
        row_sb = sb("row_sb", [P, D])
        row_gb = sb("row_gb", [P, D])
        row_b2g = sb("row_b2g", [P, D])
        b1_cols = sb("b1_cols", [P, IB])
        ident = sb("ident2", [P, P])
        stats = sb("stats2", [P, 2, 6])
        mean_var = sb("mean_var2", [P, 2, 2])
        rstd = sb("rstd2", [P, 2, 1])
        minus_half = sb("minus_half2", [P, 1])

        a_ps = [psum(f"a_ps{j}") for j in range(2)]
        z_ps = [psum(f"z_ps{j}") for j in range(GT)]
        ln_ps = psum("ln_ps")

        const_in = sem("ffn_tables_loaded")
        stage_in = [sem(f"ffn_stage{j}_loaded") for j in range(2)]
        hi_made = sem("ffn_weight_hi_made")
        w_made = sem("ffn_weight_split")
        x_in = [sem(f"x1_{j}_loaded") for j in range(2)]
        out_done = [sem(f"out_{j}_stored") for j in range(2)]
        ln_rows_in = sem("ffn_ln_rows_loaded")
        gb_in = sem("gb_loaded")
        bn_done = sem("ffn_bn_done")
        mv_done = sem("ffn_mean_var_done")
        scaled = sem("ffn_x_scaled")
        normed = sem("ffn_x_normed")
        half_set = sem("ffn_minus_half_set")
        eps_done = sem("ffn_eps_added")
        rstd_done = sem("ffn_rstd_done")
        ln_turned = sem("ffn_ln_turned")
        hT_hi_done = sem("h2T_hi_done")
        hT_lo_done = sem("h2T_lo_done")
        a_done = sem("a_done")
        relu_done = sem("relu_done")
        a_lo_done = sem("a_lo_done")
        up_used = sem("aT_used")
        z_done = sem("z_done")
        z_out = sem("z_gated_done")
        biased = sem("residual_biased")
        summed = sem("out_summed")

        block = ctx.enter_context(nc.Block())
        PIECES = 2 * KB

        def groups(engine, body):
            body(0, 0, "first")
            body(0, 1, "middle")
            with engine.Fori(1, B - 1) as b:
                body(b, 0, "middle")
                body(b, 1, "middle")
            body(B - 1, 0, "middle")
            body(B - 1, 1, "last")

        def after(b, g):
            return (b, 1) if g == 0 else (b + 1, 0)

        def tiles(b, g):
            return b * (GROUPS * GT) + g * GT

        @block.sync
        def _(sp):
            def load_group(b, g):
                if not (isinstance(b, int) and b == 0):
                    sp.wait_ge(out_done[g], b * 16)
                sp.dma_start(x[:, g, :, :], x1_groups[b, g]).then_inc(x_in[g], 16)

            def load_ln_rows(b):
                if not (isinstance(b, int) and b == 0):
                    sp.wait_ge(normed, b * (GROUPS * GT))
                    sp.wait_ge(biased, b * (GROUPS * GT))
                for r, row in ((CB, row_cb), (SB, row_sb), (B2G, row_b2g)):
                    sp.dma_start(row[:], mod_table[b, r, :].partition_broadcast(P)).then_inc(ln_rows_in, 16)

            def load_gb(b):
                if not (isinstance(b, int) and b == 0):
                    sp.wait_ge(z_out, b * (GROUPS * GT))
                sp.dma_start(row_gb[:], mod_table[b, GB, :].partition_broadcast(P)).then_inc(gb_in, 16)

            def store(b, g):
                wait_alone(sp, summed, tiles(b, g) + GT, gb_in, 16)
                sp.dma_start(out_groups[b, g], x[:, g, :, :]).then_inc(out_done[g], 16)

            sp.dma_start(ident[:], t["ident"]).then_inc(const_in, 16)
            sp.dma_start(b1_cols[:], t["b1"].rearrange("(i p) -> p i", p=P),
                         allow_slow_non_contiguous=True).then_inc(const_in, 16)
            for j in range(PIECES):
                if j >= 2:
                    sp.wait_ge(w_made, j - 1)
                stage = x[:, j % 2, :, :].rearrange("p i d -> p (i d)")
                if j < KB:
                    src = t["W1"][j * P:(j + 1) * P, :]
                else:
                    stage = x[:, j % 2, :, :]
                    src = t["W2"].rearrange("(q i p) d -> q p i d", p=P, i=GT)[j - KB]
                sp.dma_start(stage, src).then_inc(stage_in[j % 2], 16)
            sp.wait_ge(w_made, PIECES)
            load_ln_rows(0)
            load_gb(0)
            load_group(0, 0)
            load_group(0, 1)

            def body(b, g, kind):
                if kind != "first":
                    pb, pg = (b, 0) if g == 1 else (b - 1, 1)
                    store(pb, pg)
                    if g == 0:
                        load_gb(b)
                        load_group(b, 1)
                    elif not (isinstance(b, int) and b == B - 1):
                        load_group(b + 1, 0)
                if g == 0 and not (isinstance(b, int) and b == B - 1):
                    load_ln_rows(b + 1)
            groups(sp, body)
            store(B - 1, 1)
            for j in range(2):
                sp.wait_ge(out_done[j], 16 * B)

        @block.tensor
        def _(pe):
            def three(out_ps, a_hi, a_lo, b_hi, b_lo, start, stop):
                pe.matmul(out_ps, a_hi, b_hi, start=start, stop=False)
                pe.matmul(out_ps, a_hi, b_lo, start=False, stop=False)
                return pe.matmul(out_ps, a_lo, b_hi, start=False, stop=stop)

            def turn(b, g, j):
                n = tiles(b, g) + j
                pe.wait_ge(normed, n + 1)
                if not (isinstance(n, int) and n == 0):
                    pe.wait_ge(hT_lo_done, n)
                for kb in range(KB):
                    ins = pe.transpose(ln_ps[:, kb * P:(kb + 1) * P], xn[:, j % 2, kb * P:(kb + 1) * P], ident[:])
                ins.then_inc(ln_turned, 1)

            def up(b, g, i):
                n = b * (GROUPS * IB) + g * IB + i
                if i == 0:
                    pe.wait_ge(hT_lo_done, tiles(b, g) + GT)
                if not (isinstance(n, int) and n < 2):
                    pe.wait_ge(relu_done, n - 1)
                for kb in range(KB):
                    ins = three(a_ps[i % 2][:], w1_hi[:, kb, i * P:(i + 1) * P], w1_lo[:, kb, i * P:(i + 1) * P],
                                hT_hi[:, g, kb, :], hT_lo[:, g, kb, :], kb == 0, kb == KB - 1)
                ins.then_inc(a_done, 1)

            def down(b, g, i):
                n = b * (GROUPS * IB) + g * IB + i
                pe.wait_ge(a_lo_done, n + 1)
                for j in range(GT):
                    if i == 0 and not (isinstance(b, int) and b == 0 and g == 0):
                        pe.wait_ge(z_out, tiles(b, g) - GT + j + 1)
                    cols = slice(j * P, (j + 1) * P)
                    ins = three(z_ps[j][:], aT_hi[:, i % 2, cols], aT_lo[:, i % 2, cols],
                                w2_hi[:, i, :], w2_lo[:, i, :], i == 0, i == IB - 1)
                    if i == IB - 1:
                        ins.then_inc(z_done, 1)
                if i < IB - 1:
                    ins.then_inc(up_used, 1)

            pe.wait_ge(const_in, 32)
            pe.wait_ge(w_made, PIECES)
            for j in range(GT):
                turn(0, 0, j)

            def body(b, g, kind):
                for i in range(IB):
                    up(b, g, i)
                    if i > 0:
                        down(b, g, i - 1)
                    elif kind != "first":
                        pb, pg = (b, 0) if g == 1 else (b - 1, 1)
                        down(pb, pg, IB - 1)
                    if i in LN_SLOT and kind != "last":
                        turn(*after(b, g), LN_SLOT.index(i))

            groups(pe, body)
            down(B - 1, 1, IB - 1)

        @block.scalar
        def _(act):
            act.wait_ge(const_in, 32)

            def hT_hi_of(b, g, j):
                act.wait_ge(ln_turned, tiles(b, g) + j + 1)
                act.activation(hT_hi[:, g, :, j * P:(j + 1) * P], ln_ps[:].rearrange("p (k c) -> p k c", k=KB),
                               ACT.Copy).then_inc(hT_hi_done, 1)

            def activate(b, g, i):
                n = b * (GROUPS * IB) + g * IB + i
                act.wait_ge(a_done, n + 1)
                if not (isinstance(n, int) and n < 2):
                    act.wait_ge(a_lo_done, n - 1)
                act.activation(relu[:, i % 2, :], a_ps[i % 2][:], ACT.Relu, bias=b1_cols[:, i:i + 1])
                act.activation(aT_hi[:, i % 2, :], a_ps[i % 2][:], ACT.Relu,
                               bias=b1_cols[:, i:i + 1]).then_inc(relu_done, 1)

            for j in range(GT):
                hT_hi_of(0, 0, j)

            def body(b, g, kind):
                for i in range(IB):
                    activate(b, g, i)
                    if i in LN_SLOT and kind != "last":
                        hT_hi_of(*after(b, g), LN_SLOT.index(i))
            groups(act, body)

        @block.vector
        def _(dve):
            def split_weights(j):
                dve.wait_ge(stage_in[j % 2], 16 * (j // 2 + 1))
                if j < KB:
                    src = x[:, j % 2, :, :].rearrange("p i d -> p (i d)")
                    hi, lo = w1_hi[:, j, :], w1_lo[:, j, :]
                else:
                    src = x[:, j % 2, :, :]
                    q = (j - KB) * GT
                    hi, lo = w2_hi[:, q:q + GT, :], w2_lo[:, q:q + GT, :]
                dve.tensor_copy(hi, src).then_inc(hi_made, 1)
                dve.wait_ge(hi_made, j + 1)
                dve.tensor_tensor(lo, src, hi.bitcast(F32), ALU.subtract).then_inc(w_made, 1)

            def ln_stats(b, g, j):
                n = tiles(b, g) + j
                if j == 0:
                    dve.wait_ge(x_in[g], b * 16 + 16)
                dve.bn_stats(stats[:, j % 2, :], x[:, g, j, :]).then_inc(bn_done, 1)
                wait_alone(dve, bn_done, n + 1, bn_done, 1)
                dve.bn_aggr(mean_var[:, j % 2, :], stats[:, j % 2, :]).then_inc(mv_done, 1)

            def ln_apply(b, g, j):
                n = tiles(b, g) + j
                if j == 0 and g == 0:
                    dve.wait_ge(ln_rows_in, b * 48 + 48)
                dve.wait_ge(mv_done, n + 1)
                if not (isinstance(n, int) and n < 2):
                    dve.wait_ge(ln_turned, n - 1)
                dve.scalar_tensor_tensor(out=xn[:, j % 2, :], in0=x[:, g, j, :], scalar=mean_var[:, j % 2, 0:1],
                                         in1=row_cb[:], op0=ALU.subtract, op1=ALU.mult).then_inc(scaled, 1)
                dve.wait_ge(scaled, n + 1)
                dve.wait_ge(rstd_done, n + 1)
                dve.scalar_tensor_tensor(out=xn[:, j % 2, :], in0=xn[:, j % 2, :], scalar=rstd[:, j % 2, :],
                                         in1=row_sb[:], op0=ALU.mult, op1=ALU.add).then_inc(normed, 1)

            def hT_lo_of(b, g, j):
                cols = slice(j * P, (j + 1) * P)
                dve.wait_ge(hT_hi_done, tiles(b, g) + j + 1)
                dve.tensor_tensor(hT_lo[:, g, :, cols], ln_ps[:].rearrange("p (k c) -> p k c", k=KB),
                                  hT_hi[:, g, :, cols].bitcast(F32), ALU.subtract).then_inc(hT_lo_done, 1)

            def a_low(b, g, i):
                n = b * (GROUPS * IB) + g * IB + i
                dve.wait_ge(relu_done, n + 1)
                dve.tensor_tensor(aT_lo[:, i % 2, :], relu[:, i % 2, :], aT_hi[:, i % 2, :].bitcast(F32),
                                  ALU.subtract).then_inc(a_lo_done, 1)

            def gate(b, g, j):
                n = tiles(b, g) + j
                dve.wait_ge(z_done, n + 1)
                if j == 0 and g == 0:
                    dve.wait_ge(gb_in, b * 16 + 16)
                if not (isinstance(n, int) and n < 2):
                    dve.wait_ge(summed, n - 1)
                dve.tensor_tensor(gated[:, j % 2, :], z_ps[j][:], row_gb[:], ALU.mult).then_inc(z_out, 1)

            for j in range(PIECES):
                split_weights(j)
            ln_stats(0, 0, 0)
            for j in range(GT):
                ln_apply(0, 0, j)
                if j + 1 < GT:
                    ln_stats(0, 0, j + 1)
                hT_lo_of(0, 0, j)

            def body(b, g, kind):
                for i in range(IB):
                    a_low(b, g, i)
                    if i == 0 and kind != "first":
                        pb, pg = (b, 0) if g == 1 else (b - 1, 1)
                        for j in range(GT):
                            gate(pb, pg, j)
                    if kind != "last":
                        if i + 2 in LN_SLOT:
                            ln_stats(*after(b, g), LN_SLOT.index(i + 2))
                        if i + 1 in LN_SLOT:
                            ln_apply(*after(b, g), LN_SLOT.index(i + 1))
                        if i in LN_SLOT:
                            hT_lo_of(*after(b, g), LN_SLOT.index(i))
            groups(dve, body)
            for j in range(GT):
                gate(B - 1, 1, j)

        @block.gpsimd
        def _(pool):
            pool.memset(minus_half[:], -0.5).then_inc(half_set, 1)
            pool.wait_ge(half_set, 1)

            def inverse_deviation(b, g, j):
                n = tiles(b, g) + j
                wait_alone(pool, mv_done, n + 1, half_set, 1)
                pool.tensor_scalar(rstd[:, j % 2, :], mean_var[:, j % 2, 1:2], EPS, None, ALU.add).then_inc(eps_done, 1)
                pool.wait_ge(eps_done, n + 1)
                pool.tensor_tensor(rstd[:, j % 2, :], rstd[:, j % 2, :], minus_half[:], ALU.pow).then_inc(rstd_done, 1)

            def bias(b, g, j):
                pool.wait_ge(normed, tiles(b, g) + j + 1)
                pool.tensor_tensor(x[:, g, j, :], x[:, g, j, :], row_b2g[:], ALU.add).then_inc(biased, 1)

            def residual(b, g, j):
                n = tiles(b, g) + j
                pool.wait_ge(z_out, n + 1)
                pool.wait_ge(biased, n + 1)
                pool.tensor_tensor(x[:, g, j, :], x[:, g, j, :], gated[:, j % 2, :], ALU.add).then_inc(summed, 1)

            for j in range(GT):
                inverse_deviation(0, 0, j)
                bias(0, 0, j)

            def body(b, g, kind):
                if kind != "first":
                    pb, pg = (b, 0) if g == 1 else (b - 1, 1)
                    for j in range(GT):
                        residual(pb, pg, j)
                if kind != "last":
                    for j in range(GT):
                        inverse_deviation(*after(b, g), j)
                        bias(*after(b, g), j)
            groups(pool, body)
            for j in range(GT):
                residual(B - 1, 1, j)


def build(nc, t, out):
    mod_table = nc.dram_tensor("mod_table", [B, 7, D], F32, kind="Internal").ap()
    x1 = nc.dram_tensor("x1", [B, T, D], F32, kind="Internal").ap()
    with ExitStack() as ctx:
        def sb(name, shape, dt=F32):
            return ctx.enter_context(nc.sbuf_tensor(name, shape, dt))

        w = {
            "wqkv_hi": sb("wqkv_hi", [P, KB, H, QKV], F32R), "wqkv_lo": sb("wqkv_lo", [P, KB, H, QKV], F32R),
            "wo_hi": sb("wo_hi", [P, H, D], F32R), "wo_lo": sb("wo_lo", [P, H, D], F32R),
            "cos": sb("cos", [P, NT, ROT]), "sin": sb("sin", [P, NT, ROT]),
            "ident": sb("ident", [P, P]), "ident16": sb("ident16", [P, P], BF16), "mask16": sb("mask16", [P, P], BF16),
        }
        prepare(nc, t, mod_table, w)
        attention(nc, t, mod_table, x1, w)
    ffn(nc, t, mod_table, x1, out)


def tables():
    freqs = np.power(np.float32(10000.0), -np.arange(HALF, dtype=np.float32) / np.float32(HALF)).astype(np.float32)
    radians = np.arange(T, dtype=np.float32)[:, None] * freqs[None, :]
    cos, sin = np.cos(radians).astype(np.float32), np.sin(radians).astype(np.float32)
    by_tile = lambda a: np.ascontiguousarray(a.reshape(NT, P, ROT).transpose(1, 0, 2))
    upper = np.triu(np.ones((P, P), np.float32), 1)
    return {
        "cos": by_tile(np.concatenate([cos, cos], 1)), "sin": by_tile(np.concatenate([-sin, sin], 1)), "ident": np.eye(P, dtype=np.float32),
        "mask": upper * np.float32(MASKED),
    }


_NAMES = {"L0_attn_x": "x", "L0_attn_wq": "wq", "L0_attn_wk": "wk", "L0_attn_wv": "wv", "L0_attn_wo": "wo",
          "L0_ffn_W1": "W1", "L0_ffn_b1": "b1", "L0_ffn_W2": "W2", "L0_ffn_b2": "b2", "L0_c": "c", "L0_wmod": "wmod"}


def kernel(**inputs):
    import concourse.bacc as bacc
    from concourse.bass_utils import run_bass_kernel_spmd

    nc = bacc.Bacc("TRN2", target_bir_lowering=False, num_devices=1)
    arrays, t = {}, {}
    named = {short: np.ascontiguousarray(inputs[name]) for name, short in _NAMES.items()}
    for short, a in {**named, **tables()}.items():
        arrays[f"in_{short}"] = a
        t[short] = nc.dram_tensor(f"in_{short}", a.shape, mybir.dt.from_np(a.dtype), kind="ExternalInput").ap()
    out = nc.dram_tensor("out", (B, T, D), F32, kind="ExternalOutput").ap()
    build(nc, t, out)
    r = run_bass_kernel_spmd(nc, [arrays], core_ids=[0])
    return r.results[0]["out"]
```

```python
from contextlib import ExitStack

import numpy as np

import concourse.bass as bass
from concourse import mybir

F32 = mybir.dt.float32
F32R = mybir.dt.float32r
BF16 = mybir.dt.bfloat16
ALU = mybir.AluOpType
ACT = mybir.ActivationFunctionType
AX = mybir.AxisListType

P = 128
B, T, D = 8, 1024, 512
H, DH = 4, 128
INTER = 2048
KB = D // P
NT = T // P
IB = INTER // P
ROT = DH // 2
HALF = ROT // 2
QKV = 3 * DH
EPS = 1e-5
GATE_MIN = 0.25
MASKED = -1e30
STEPS = H * NT
CHUNKS = NT + NT // 2
GT = 4
GROUPS = NT // GT
SA, CA, GA, SB, CB, GB, B2G = range(7)
WO_STEP = [1, 2, 4, 5, 7, 8, 10, 11]
LN_STEP = [17, 19, 21, 23, 25, 26, 28, 30]
TAIL_STEPS = 14
W1_PIECE = 1024
W1_PIECES = KB * INTER // W1_PIECE
W1_STAGES = KB * T // W1_PIECE
W1_LOAD = {"last": [24, 24, 24, 24, 27, 29, 31], "tail": [2]}
W1_SPLIT = {"last": [25, 27, 29, 31], "tail": [1, 4, 7, 10]}


def p_column(i):
    return P * (i * (i + 1) // 2)


def chunks_of(i):
    return [2 * i, 2 * i + 1] if i < NT // 2 else [NT // 2 + i]


class Step:

    def __init__(self, b, k, kind):
        self.b, self.k, self.kind = b, k, kind
        self.h, self.i = divmod(k, NT)
        self.n = b * STEPS + k
        self.scores = kind != "tail"
        self.project = self.has_project(k)
        self.natural = (kind not in ("first", "tail")) if k == 0 else self.has_project(k - 1)
        self.turn = kind != "tail" if k < 2 else self.has_project(k - 2)
        self.out = [j for j, s in enumerate(WO_STEP) if s == k] if kind != "first" else []

    def has_project(self, k):
        return self.kind in ("first", "middle") or (self.kind == "last" and k < STEPS - NT)

    def has_chunk(self, s):
        if s < NT:
            return not (self.kind == "first" and self.h == 0 or self.kind == "tail" and self.h > 0)
        return self.kind != "tail"

    def chunk_count(self, s):
        return self.b * (H * CHUNKS) + self.h * CHUNKS + s + 1 - NT

    def chunk(self, s):
        if s < 0:
            return 0, GT - 1, (self.h + 1) % 2
        if s < NT:
            return 1, s, (self.h + 1) % 2
        return 0, s - NT, self.h % 2

    def w1_pieces(self, schedule):
        before = 0 if self.kind == "last" else len(schedule["last"])
        return [before + m for m, k in enumerate(schedule.get(self.kind, [])) if k == self.k]

    def ln(self, step):
        known = self.kind in ("first", "middle") and self.k - step in LN_STEP
        return LN_STEP.index(self.k - step) if known else None


def batch_rows(engine, body):
    body(0, "first", STEPS)
    with engine.Fori(1, B - 1) as b:
        body(b, "middle", STEPS)
    body(B - 1, "last", STEPS)
    body(B, "tail", TAIL_STEPS)


def wait_alone(engine, semaphore, value, passed, at_least):
    value = value if isinstance(value, int) else engine.to_reg(value)
    engine.wait_ge(passed, at_least)
    engine.wait_ge(semaphore, value)


def prepare(nc, t, mod_table, w):
    with ExitStack() as ctx:
        def sb(name, shape, dt=F32):
            return ctx.enter_context(nc.sbuf_tensor(name, shape, dt))

        def sem(name):
            return ctx.enter_context(nc.semaphore(name))

        stage = sb("weight_stage", [P, 2, 4, H, DH])
        wmod = sb("wmod_stage", [P, KB, 6 * D])
        mask = sb("mask", [P, P])
        c_cols = sb("c_cols", [P, KB, B])
        e_cols = sb("e_cols", [P, KB, B])
        d_cols = sb("d_cols", [P, KB, B])
        r_cols = sb("r_cols", [P, KB, B])
        silu = sb("silu", [P, KB, B])
        rows = sb("mod_rows", [B, 7, D])
        b2_rows = sb("b2_rows", [B, D])
        mag = sb("gate_magnitude", [B, 2, D])
        sign = sb("gate_sign", [B, 2, D])
        acc = [ctx.enter_context(nc.psum_tensor(f"mod_acc{r}", [P, D], F32)) for r in range(6)]

        c_in = sem("c_loaded")
        const_in = sem("tables_loaded")
        wmod_in = [sem(f"wmod{k}_loaded") for k in range(KB)]
        stage_in = [sem(f"stage{j}_loaded") for j in range(2)]
        split = sem("weights_split")
        exp_done = sem("exp_done")
        chain = sem("vector_chain")
        silu_done = sem("silu_done")
        acc_done = sem("mod_rows_multiplied")
        rows_done = sem("mod_rows_done")
        stored = sem("mod_rows_stored")
        sources = [t["wq"], t["wk"], t["wv"]]

        block = ctx.enter_context(nc.Block())

        @block.sync
        def _(sp):
            for kb in range(KB):
                sp.dma_start(c_cols[:, kb, :], t["c"][:, kb * P:(kb + 1) * P].rearrange("b p -> p b"),
                             allow_slow_non_contiguous=True).then_inc(c_in, 16)
            sp.dma_start(w["cos"][:], t["cos"]).then_inc(const_in, 16)
            sp.dma_start(w["sin"][:], t["sin"]).then_inc(const_in, 16)
            sp.dma_start(w["ident"][:], t["ident"]).then_inc(const_in, 16)
            sp.dma_start(mask[:], t["mask"]).then_inc(const_in, 16)
            sp.dma_start(b2_rows[:], t["b2"].rearrange("(a d) -> a d", a=1).to_broadcast([B, D])).then_inc(const_in, 16)
            for k in range(KB):
                sp.dma_start(wmod[:, k, :], t["wmod"][k * P:(k + 1) * P, :]).then_inc(wmod_in[k], 16)
            sp.wait_ge(rows_done, 1)
            sp.dma_start(mod_table, rows[:]).then_inc(stored, 16)
            sp.wait_ge(stored, 16)

        @block.scalar
        def _(act):
            for j in range(4):
                if j >= 2:
                    act.wait_ge(split, 2 * (j - 1))
                for kb in range(KB):
                    if j < 3:
                        src = sources[j][:, kb * P:(kb + 1) * P, :].rearrange("h p k -> p h k")
                        act.dma_start(stage[:, j % 2, kb, :, :], src).then_inc(stage_in[j % 2], 16)
                    else:
                        act.dma_start(stage[:, 1, kb, :, :].rearrange("p h k -> p (h k)"),
                                      t["wo"][kb * P:(kb + 1) * P, :]).then_inc(stage_in[1], 16)
                if j == 1:
                    act.wait_ge(c_in, 16 * KB)
                    act.activation(e_cols[:], c_cols[:], ACT.Exp, scale=-1.0).then_inc(exp_done, 1)

        @block.vector
        def _(dve):
            n = [0]

            def link(ins):
                n[0] += 1
                ins.then_inc(chain, 1)
                dve.wait_ge(chain, n[0])

            def weights(j):
                dve.wait_ge(stage_in[j % 2], 16 * KB * (j // 2 + 1))
                for kb in range(KB):
                    src = stage[:, j % 2, kb, :, :]
                    if j < 3:
                        hi = w["wqkv_hi"][:, kb, :, j * DH:(j + 1) * DH]
                        lo = w["wqkv_lo"][:, kb, :, j * DH:(j + 1) * DH]
                    else:
                        hi = w["wo_hi"][:, kb, :].rearrange("p (h k) -> p h k", h=H)
                        lo = w["wo_lo"][:, kb, :].rearrange("p (h k) -> p h k", h=H)
                    f = 1.0 / DH if j == 0 else 1.0
                    if f == 1.0:
                        link(dve.tensor_copy(hi, src))
                    else:
                        link(dve.tensor_scalar(hi, src, f, None, ALU.mult))
                    ins = dve.scalar_tensor_tensor(out=lo, in0=src, scalar=f, in1=hi.bitcast(F32),
                                                   op0=ALU.mult, op1=ALU.subtract)
                ins.then_inc(split, 2)

            dve.wait_ge(const_in, 16 * 5)
            dve.tensor_copy(w["ident16"][:], w["ident"][:])
            dve.tensor_copy(w["mask16"][:], mask[:])
            dve.wait_ge(exp_done, 1)
            link(dve.tensor_scalar(d_cols[:], e_cols[:], 1.0, None, ALU.add))
            link(dve.reciprocal(r_cols[:], d_cols[:]))
            dve.tensor_tensor(silu[:], c_cols[:], r_cols[:], ALU.mult).then_inc(silu_done, 1)
            for j in range(4):
                weights(j)
            dve.wait_ge(acc_done, 1)
            for r in (SA, SB):
                dve.tensor_copy(rows[:, r, :], acc[r][0:B, :])
            for r in (CA, CB):
                dve.tensor_scalar(rows[:, r, :], acc[r][0:B, :], 1.0, None, ALU.add)
            for j, r in enumerate((GA, GB)):
                dve.tensor_scalar(mag[:, j, :], acc[r][0:B, :], -1.0, None, ALU.mult)
                link(dve.tensor_scalar(sign[:, j, :], acc[r][0:B, :], 0.0, 2.0, ALU.is_ge, ALU.mult))
                link(dve.tensor_tensor(mag[:, j, :], acc[r][0:B, :], mag[:, j, :], ALU.max))
                link(dve.tensor_scalar(mag[:, j, :], mag[:, j, :], GATE_MIN, None, ALU.max))
                link(dve.scalar_tensor_tensor(out=rows[:, r, :], in0=sign[:, j, :], scalar=-1.0,
                                              in1=mag[:, j, :], op0=ALU.add, op1=ALU.mult))
            dve.tensor_tensor(rows[:, B2G, :], rows[:, GB, :], b2_rows[:], ALU.mult).then_inc(rows_done, 1)

        @block.tensor
        def _(pe):
            pe.wait_ge(silu_done, 1)
            for k in range(KB):
                pe.wait_ge(wmod_in[k], 16)
                for r in range(6):
                    ins = pe.matmul(acc[r][0:B, :], silu[:, k, :], wmod[:, k, r * D:(r + 1) * D],
                                    start=(k == 0), stop=(k == KB - 1))
            ins.then_inc(acc_done, 1)


def attention(nc, t, mod_table, x1, w, w1):
    x_tiles = t["x"].rearrange("b (i p) d -> b i p d", p=P)
    x1_tiles = x1.rearrange("b (i p) d -> b i p d", p=P)

    with ExitStack() as ctx:
        def sb(name, shape, dt=F32):
            return ctx.enter_context(nc.sbuf_tensor(name, shape, dt))

        def psum(name, shape):
            return ctx.enter_context(nc.psum_tensor(name, shape, F32))

        def sem(name):
            return ctx.enter_context(nc.semaphore(name))

        def pair(name, shape):
            return sb(name + "_hi", shape, F32R), sb(name + "_lo", shape, F32R)

        wqkv_hi, wqkv_lo, wo_hi, wo_lo = w["wqkv_hi"], w["wqkv_lo"], w["wo_hi"], w["wo_lo"]
        ident = w["ident"]
        hT_hi, hT_lo = w["hT_hi"], w["hT_lo"]
        qT_hi, qT_lo = pair("qT", [P, T])
        kT_hi, kT_lo = pair("kT", [P, 2, T])
        v_hi, v_lo = pair("v", [P, 2, NT, DH])
        pT_hi, pT_lo = pair("pT", [P, 2, GT * P])
        oT_tile_hi, oT_tile_lo = pair("oT_tile", [P, H, P])
        probs = sb("probs", [P, p_column(NT)])
        oT = sb("oT", [P, H, T])
        x_ln = sb("x_ln", [P, 2, D])
        x_res = sb("x_res", [P, 2, D])
        gated = sb("gated", [P, D])
        nat = sb("qkv_natural", [P, 2, QKV])
        by_cos = sb("by_cos", [P, 2, ROT])
        by_sin = sb("by_sin", [P, 2, ROT])
        row_ca = sb("row_ca", [P, D])
        row_sa = sb("row_sa", [P, D])
        row_ga = sb("row_ga", [P, D])
        stats = sb("stats", [P, 2, 6])
        mean_var = sb("mean_var", [P, 2, 2])
        rstd = sb("rstd", [P, 2, 1])
        minus_half = sb("minus_half", [P, 1])
        neg_max = sb("neg_max", [P, NT])
        row_sum = sb("row_sum", [P, NT])
        inv_sum = sb("inv_sum", [P, NT])

        s_ps = psum("scores_ps", [P, T])
        qkv_ps = psum("qkv_ps", [P, 512])
        turn_ps = psum("turn_ps", [P, 512])
        pT_ps = [psum(f"pT_ps{j}", [P, GT * P]) for j in range(2)]
        o_ps = psum("o_ps", [P, GT * P])
        mix_ps = psum("mix_ps", [P, D])

        scores_done = sem("scores_done")
        qkv_done = sem("qkv_done")
        turned = sem("qk_turned")
        pT_done = sem("pT_done")
        pv_done = sem("pv_done")
        ln_turned = sem("ln_turned")
        y_done = sem("y_done")
        nat_copied = sem("nat_copied")
        exp_done = sem("exp_done")
        qk_hi_done = sem("qk_hi_done")
        pT_hi_done = sem("pT_hi_done")
        oT_done = sem("oT_done")
        hT_hi_done = sem("hT_hi_done")
        ropes_done = sem("ropes_done")
        v_lo_done = sem("v_lo_done")
        max_done = sem("max_done")
        inv_done = sem("inv_done")
        qk_lo_done = sem("qk_lo_done")
        pT_lo_done = sem("pT_lo_done")
        hT_lo_done = sem("hT_lo_done")
        bn_done = sem("bn_done")
        mv_done = sem("mean_var_done")
        scaled = sem("x_scaled")
        normed = sem("x_normed")
        gated_done = sem("gated_done")
        half_set = sem("minus_half_set")
        rotated = sem("rotated")
        v_hi_done = sem("v_hi_done")
        probs_done = sem("probs_normalised")
        last_probs_done = sem("last_probs_normalised")
        eps_done = sem("eps_added")
        rstd_done = sem("rstd_done")
        oT_hi_done = sem("oT_tile_hi_done")
        oT_lo_done = sem("oT_tile_lo_done")
        x1_done = sem("x1_done")
        x_ln_in = [sem(f"x_ln{j}_loaded") for j in range(2)]
        x_res_in = [sem(f"x_res{j}_loaded") for j in range(2)]
        x1_out = [sem(f"x1_{j}_stored") for j in range(2)]
        w1_in = [sem(f"w1_stage{j}_loaded") for j in range(W1_STAGES)]
        w1_hi_made = sem("w1_hi_made")
        w1_lo_made = sem("w1_lo_made")
        ln_rows_in = sem("ln_rows_loaded")
        ga_in = sem("ga_loaded")

        def w1_piece(matrix, m):
            kb, c = divmod(m * W1_PIECE, INTER)
            return matrix[:, kb, c:c + W1_PIECE]

        block = ctx.enter_context(nc.Block())

        @block.sync
        def _(sp):
            def load_w1(m):
                if m == 0:
                    sp.wait_ge(qkv_done, B * STEPS)
                if m >= W1_STAGES:
                    sp.wait_ge(w1_lo_made, m - W1_STAGES + 1)
                kb, c = divmod(m * W1_PIECE, INTER)
                sp.dma_start(w1["stage"][:, m % W1_STAGES, :],
                             t["W1"][kb * P:(kb + 1) * P, c:c + W1_PIECE]).then_inc(w1_in[m % W1_STAGES], 16)

            def load_ln(b, i):
                if not (isinstance(b, int) and b == 0 and i < 2):
                    sp.wait_ge(ln_turned, b * NT + i - 1)
                sp.dma_start(x_ln[:, i % 2, :], x_tiles[b, i]).then_inc(x_ln_in[i % 2], 16)

            def load_ln_rows(b):
                if not (isinstance(b, int) and b == 0):
                    sp.wait_ge(normed, b * NT)
                sp.dma_start(row_ca[:], mod_table[b, CA, :].partition_broadcast(P)).then_inc(ln_rows_in, 16)
                sp.dma_start(row_sa[:], mod_table[b, SA, :].partition_broadcast(P)).then_inc(ln_rows_in, 16)

            def load_ga(b):
                if not (isinstance(b, int) and b == 0):
                    sp.wait_ge(gated_done, b * NT)
                sp.dma_start(row_ga[:], mod_table[b, GA, :].partition_broadcast(P)).then_inc(ga_in, 16)

            def load_res(b, i):
                if not (isinstance(b, int) and b == 0 and i < 2):
                    sp.wait_ge(x1_out[i % 2], b * (NT // 2 * 16) + i // 2 * 16)
                sp.dma_start(x_res[:, i % 2, :], x_tiles[b, i]).then_inc(x_res_in[i % 2], 16)

            def store(b, i):
                wait_alone(sp, x1_done, b * NT + i + 1, ga_in, 16)
                sp.dma_start(x1_tiles[b, i], x_res[:, i % 2, :]).then_inc(x1_out[i % 2], 16)

            load_ln_rows(0)
            for i in range(NT):
                load_ln(0, i)

            def body(b, kind, steps):
                for k in range(steps):
                    st = Step(b, k, kind)
                    if k == 1 and kind in ("first", "middle"):
                        load_ln_rows(b + 1)
                    for j in [j for j, s in enumerate(WO_STEP) if kind != "first" and s + 1 == k]:
                        store(b - 1, j)
                        if j + 2 < NT:
                            load_res(b - 1, j + 2)
                    if k == WO_STEP[-1] + 2 and kind != "tail":
                        load_ga(b)
                        load_res(b, 0)
                        load_res(b, 1)
                    t_ln = st.ln(-3)
                    if t_ln is not None:
                        load_ln(b + 1, t_ln)
                    for m in st.w1_pieces(W1_LOAD):
                        load_w1(m)

            batch_rows(sp, body)
            for j in range(2):
                sp.wait_ge(x1_out[j], 16 * B * NT // 2)

        @block.tensor
        def _(pe):
            def three(out, a_hi, a_lo, b_hi, b_lo, start, stop):
                pe.matmul(out, a_hi, b_hi, start=start, stop=False)
                pe.matmul(out, a_hi, b_lo, start=False, stop=False)
                return pe.matmul(out, a_lo, b_hi, start=False, stop=stop)

            def project(b, h, i, kbs):
                if kbs[0] == 0:
                    pe.wait_ge(hT_lo_done, b * NT + i + 1)
                    if not (isinstance(b, int) and b == 0 and h == 0 and i == 0):
                        pe.wait_ge(nat_copied, b * STEPS + h * NT + i)
                cols = slice(i * P, (i + 1) * P)
                for kb in kbs:
                    ins = three(qkv_ps[:, 0:QKV], hT_hi[:, kb, cols], hT_lo[:, kb, cols],
                                wqkv_hi[:, kb, h, :], wqkv_lo[:, kb, h, :], kb == 0, kb == KB - 1)
                if kbs[-1] == KB - 1:
                    ins.then_inc(qkv_done, 1)

            def turn(n, i):
                pe.wait_ge(rotated, n + 1)
                if not (isinstance(n, int) and n == 0):
                    pe.wait_ge(qk_lo_done, n)
                pe.transpose(turn_ps[:, 0:P], nat[:, i % 2, 0:DH], ident[:])
                pe.transpose(turn_ps[:, P:2 * P], nat[:, i % 2, DH:2 * DH], ident[:]).then_inc(turned, 1)

            def scores(st):
                i, par = st.i, st.h % 2
                pe.wait_ge(qk_lo_done, st.n + 1)
                if not (st.kind == "first" and st.k == 0):
                    pe.wait_ge(exp_done, st.n)
                q_cols = slice(i * P, (i + 1) * P)
                for c in range(0, (i + 1) * P, 512):
                    end = min((i + 1) * P, c + 512)
                    diagonal = end == (i + 1) * P
                    ins = three(s_ps[:, c:end], qT_hi[:, q_cols], qT_lo[:, q_cols],
                                kT_hi[:, par, c:end], kT_lo[:, par, c:end], True, not diagonal)
                    if diagonal:
                        ins = pe.matmul(s_ps[:, i * P:end], w["ident16"][:], w["mask16"][:],
                                        start=False, stop=True)
                ins.then_inc(scores_done, 1)

            def slot(st, s):
                if s < CHUNKS and st.has_chunk(s):
                    group, j, _ = st.chunk(s)
                    done = (st.b * H + st.h - (1 if group == 1 else 0)) * GROUPS + group + 1
                    pe.wait_ge(probs_done, done * (GT - 1))
                    pe.wait_ge(last_probs_done, done)
                    count = st.chunk_count(s)
                    if not (st.kind == "first" and st.h == 0 and s < NT + 2):
                        pe.wait_ge(pT_lo_done, count - 2)
                    for i in range(max(j, GT * group), GT * group + GT):
                        c = p_column(i) + j * P
                        o = (i - GT * group) * P
                        ins = pe.transpose(pT_ps[s % 2][:, o:o + P], probs[:, c:c + P], ident[:])
                    ins.then_inc(pT_done, 1)
                if st.has_chunk(s - 1):
                    group, j, par = st.chunk(s - 1)
                    pe.wait_ge(pT_lo_done, st.chunk_count(s - 1))
                    if j == 0 and not (st.kind == "first" and st.h == 0):
                        before = st.b * (2 * H) + 2 * st.h + (0 if group == 0 else -1)
                        pe.wait_ge(oT_done, before)
                    c0 = max(0, j - GT * group) * P
                    buf = (s - 1) % 2
                    three(o_ps[:, c0:], v_hi[:, par, j, :], v_lo[:, par, j, :],
                          pT_hi[:, buf, c0:], pT_lo[:, buf, c0:], j == 0,
                          j == GT * group + GT - 1).then_inc(pv_done, 1)

            def turn_ln(b, i):
                pe.wait_ge(normed, b * NT + i + 1)
                if not (isinstance(b, int) and b == 0 and i == 0):
                    pe.wait_ge(hT_lo_done, b * NT + i)
                if i == 0 and not (isinstance(b, int) and b <= 1):
                    pe.wait_ge(gated_done, (b - 1) * NT)
                for kb in range(KB):
                    ins = pe.transpose(mix_ps[:, kb * P:(kb + 1) * P], x_ln[:, i % 2, kb * P:(kb + 1) * P], ident[:])
                ins.then_inc(ln_turned, 1)

            def output(b, i):
                pe.wait_ge(oT_lo_done, b * NT + i + 1)
                if i == 0:
                    if not (isinstance(b, int) and b == B - 1):
                        pe.wait_ge(hT_lo_done, (b + 2) * NT)
                else:
                    pe.wait_ge(gated_done, b * NT + i)
                for h in range(H):
                    ins = three(mix_ps[:], oT_tile_hi[:, h, :], oT_tile_lo[:, h, :],
                                wo_hi[:, h, :], wo_lo[:, h, :], h == 0, h == H - 1)
                ins.then_inc(y_done, 1)

            for i in range(NT):
                turn_ln(0, i)
                if i > 0:
                    project(0, 0, i - 1, range(KB))
                if i > 1:
                    turn(i - 2, i - 2)
            project(0, 0, NT - 1, range(KB))

            def body(b, kind, steps):
                for k in range(steps):
                    st = Step(b, k, kind)
                    i = st.i
                    nb, nh = (b + 1, 0) if st.h == H - 1 else (b, st.h + 1)
                    if kind == "tail" and k >= NT:
                        for j in st.out:
                            output(b - 1, j)
                        continue
                    if st.scores:
                        scores(st)
                    todo = chunks_of(i)
                    slot(st, todo[0])
                    if st.ln(0) is not None:
                        turn_ln(b + 1, st.ln(0))
                    if st.project:
                        project(nb, nh, i, range(0, KB // 2))
                    if st.turn:
                        turn(st.n + NT - 2, (i - 2) % NT)
                    if len(todo) > 1:
                        slot(st, todo[1])
                    if st.project:
                        project(nb, nh, i, range(KB // 2, KB))
                    for j in st.out:
                        output(b - 1, j)

            batch_rows(pe, body)

        @block.scalar
        def _(act):
            def natural(n, i):
                act.wait_ge(qkv_done, n + 1)
                if not (isinstance(n, int) and n < 2):
                    act.wait_ge(turned, n - 1)
                    act.wait_ge(v_lo_done, n - 1)
                act.activation(nat[:, i % 2, :], qkv_ps[:, 0:QKV], ACT.Copy).then_inc(nat_copied, 1)

            def v_high(n, i, par):
                act.wait_ge(nat_copied, n + 1)
                act.activation(v_hi[:, par, i, :], nat[:, i % 2, 2 * DH:QKV], ACT.Copy).then_inc(v_hi_done, 1)

            def oT_tile_hi_of(b, i):
                act.wait_ge(oT_done, b * (2 * H) + 2 * H - 1 + i // GT)
                if not (isinstance(b, int) and b == 0 and i == 0):
                    act.wait_ge(y_done, b * NT + i)
                act.activation(oT_tile_hi[:], oT[:, :, i * P:(i + 1) * P], ACT.Copy).then_inc(oT_hi_done, 1)

            def qk_hi(n, i, par):
                act.wait_ge(turned, n + 1)
                cols = slice(i * P, (i + 1) * P)
                act.activation(qT_hi[:, cols], turn_ps[:, 0:P], ACT.Copy)
                act.activation(kT_hi[:, par, cols], turn_ps[:, P:2 * P], ACT.Copy).then_inc(qk_hi_done, 1)

            def hT_hi_of(b, i):
                act.wait_ge(ln_turned, b * NT + i + 1)
                act.activation(hT_hi[:, :, i * P:(i + 1) * P], mix_ps[:].rearrange("p (k c) -> p k c", k=KB),
                               ACT.Copy).then_inc(hT_hi_done, 1)

            def w1_high(m):
                act.wait_ge(w1_in[m % W1_STAGES], 16 * (m // W1_STAGES + 1))
                act.activation(w1_piece(w1["hi"], m), w1["stage"][:, m % W1_STAGES, :],
                               ACT.Copy).then_inc(w1_hi_made, 1)

            def pT_hi_of(st, s):
                if s < CHUNKS and st.has_chunk(s):
                    group, j, _ = st.chunk(s)
                    c0 = max(0, j - GT * group) * P
                    act.wait_ge(pT_done, st.chunk_count(s))
                    act.activation(pT_hi[:, s % 2, c0:], pT_ps[s % 2][:, c0:], ACT.Copy).then_inc(pT_hi_done, 1)

            def attended(st, s):
                if st.has_chunk(s - 1):
                    group, _, _ = st.chunk(s - 1)
                    act.wait_ge(pv_done, st.chunk_count(s - 1))
                    head = (st.h - 1) % H
                    if head == 0 and not (st.kind == "first"):
                        act.wait_ge(oT_lo_done, (st.b - 1) * NT + (group + 1) * GT)
                    act.activation(oT[:, head, group * GT * P:(group + 1) * GT * P], o_ps[:],
                                   ACT.Copy).then_inc(oT_done, 1)

            def exps(st):
                i = st.i
                W = (i + 1) * P
                act.wait_ge(max_done, st.n + 1)
                act.activation(probs[:, p_column(i):p_column(i) + W], s_ps[:, 0:W], ACT.Exp,
                               bias=neg_max[:, i:i + 1], accum_out=row_sum[:, i:i + 1]).then_inc(exp_done, 1)

            for i in range(NT):
                hT_hi_of(0, i)
                if i > 0:
                    natural(i - 1, i - 1)
                    v_high(i - 1, i - 1, 0)
                if i > 1:
                    qk_hi(i - 2, i - 2, 0)
            natural(NT - 1, NT - 1)
            v_high(NT - 1, NT - 1, 0)

            def body(b, kind, steps):
                for k in range(steps):
                    st = Step(b, k, kind)
                    i = st.i
                    todo = chunks_of(i)
                    if st.natural:
                        natural(st.n + NT - 1, (i - 1) % NT)
                    if kind == "tail" and k > NT // 2:
                        for j in st.out:
                            oT_tile_hi_of(b - 1, j)
                        for m in st.w1_pieces(W1_SPLIT):
                            w1_high(m)
                        continue
                    for j in st.out:
                        oT_tile_hi_of(b - 1, j)
                    pT_hi_of(st, todo[0])
                    if i == 0:
                        attended(st, 0)
                    if i == NT // 2:
                        attended(st, NT)
                    if st.natural:
                        v_high(st.n + NT - 1, (i - 1) % NT, (st.h + (i > 0)) % 2)
                    if st.ln(0) is not None:
                        hT_hi_of(b + 1, st.ln(0))
                    if st.scores:
                        exps(st)
                    if st.turn:
                        qk_hi(st.n + NT - 2, (i - 2) % NT, (st.h + (i > 1)) % 2)
                    if len(todo) > 1:
                        pT_hi_of(st, todo[1])
                    for m in st.w1_pieces(W1_SPLIT):
                        w1_high(m)

            batch_rows(act, body)

        @block.vector
        def _(dve):
            def ropes(n, i):
                dve.wait_ge(nat_copied, n + 1)
                if not (isinstance(n, int) and n == 0):
                    dve.wait_ge(rotated, n)
                qk = nat[:, i % 2, 0:2 * DH].rearrange("p (t c) -> p t c", t=2)
                even, odd = slice(0, HALF), slice(HALF, ROT)

                def table(name, part):
                    return w[name][:, i:i + 1, part].to_broadcast([P, 2, part.stop - part.start])

                dve.tensor_tensor(by_cos[:], qk[:, :, 0:ROT], table("cos", slice(0, ROT)), ALU.mult)
                dve.tensor_tensor(by_sin[:, :, even], qk[:, :, odd], table("sin", even), ALU.mult)
                dve.tensor_tensor(by_sin[:, :, odd], qk[:, :, even], table("sin", odd), ALU.mult).then_inc(ropes_done, 1)

            def rotate(n, i):
                dve.wait_ge(ropes_done, n + 1)
                qk = nat[:, i % 2, 0:2 * DH].rearrange("p (t c) -> p t c", t=2)
                dve.tensor_tensor(qk[:, :, 0:ROT], by_cos[:], by_sin[:], ALU.add).then_inc(rotated, 1)

            def v_low(n, i, par):
                dve.wait_ge(v_hi_done, n + 1)
                dve.tensor_tensor(v_lo[:, par, i, :], nat[:, i % 2, 2 * DH:QKV], v_hi[:, par, i, :].bitcast(F32),
                                  ALU.subtract).then_inc(v_lo_done, 1)

            def qk_lo(n, i, par):
                dve.wait_ge(qk_hi_done, n + 1)
                cols = slice(i * P, (i + 1) * P)
                dve.tensor_tensor(qT_lo[:, cols], turn_ps[:, 0:P], qT_hi[:, cols].bitcast(F32), ALU.subtract)
                dve.tensor_tensor(kT_lo[:, par, cols], turn_ps[:, P:2 * P], kT_hi[:, par, cols].bitcast(F32),
                                  ALU.subtract).then_inc(qk_lo_done, 1)

            def hT_lo_of(b, i):
                dve.wait_ge(hT_hi_done, b * NT + i + 1)
                dve.tensor_tensor(hT_lo[:, :, i * P:(i + 1) * P], mix_ps[:].rearrange("p (k c) -> p k c", k=KB),
                                  hT_hi[:, :, i * P:(i + 1) * P].bitcast(F32), ALU.subtract).then_inc(hT_lo_done, 1)

            def pT_lo_of(st, s):
                if s < CHUNKS and st.has_chunk(s):
                    group, j, _ = st.chunk(s)
                    c0 = max(0, j - GT * group) * P
                    dve.wait_ge(pT_hi_done, st.chunk_count(s))
                    dve.tensor_tensor(pT_lo[:, s % 2, c0:], pT_ps[s % 2][:, c0:], pT_hi[:, s % 2, c0:].bitcast(F32),
                                      ALU.subtract).then_inc(pT_lo_done, 1)

            def maxima(st):
                i = st.i
                dve.wait_ge(scores_done, st.n + 1)
                dve.tensor_reduce(neg_max[:, i:i + 1], s_ps[:, 0:(i + 1) * P], AX.X, ALU.max,
                                  negate=True).then_inc(max_done, 1)

            def inverse(st):
                dve.wait_ge(exp_done, st.n + 1)
                dve.reciprocal(inv_sum[:, st.i:st.i + 1], row_sum[:, st.i:st.i + 1]).then_inc(inv_done, 1)

            def normalise(st):
                i = st.i
                dve.wait_ge(inv_done, st.n + 1)
                p = probs[:, p_column(i):p_column(i + 1)]
                dve.tensor_scalar(p, p, inv_sum[:, i:i + 1], None, ALU.mult).then_inc(last_probs_done, 1)

            def ln_stats(b, i):
                dve.wait_ge(x_ln_in[i % 2], b * (NT // 2 * 16) + (i // 2 + 1) * 16)
                dve.bn_stats(stats[:, i % 2, :], x_ln[:, i % 2, :]).then_inc(bn_done, 1)
                wait_alone(dve, bn_done, b * NT + i + 1, bn_done, 1)
                dve.bn_aggr(mean_var[:, i % 2, :], stats[:, i % 2, :]).then_inc(mv_done, 1)

            def ln_apply(b, i):
                x = x_ln[:, i % 2, :]
                if i == 0:
                    dve.wait_ge(ln_rows_in, b * 32 + 32)
                dve.wait_ge(mv_done, b * NT + i + 1)
                dve.scalar_tensor_tensor(out=x, in0=x, scalar=mean_var[:, i % 2, 0:1], in1=row_ca[:],
                                         op0=ALU.subtract, op1=ALU.mult).then_inc(scaled, 1)
                dve.wait_ge(scaled, b * NT + i + 1)
                dve.wait_ge(rstd_done, b * NT + i + 1)
                dve.scalar_tensor_tensor(out=x, in0=x, scalar=rstd[:, i % 2, :], in1=row_sa[:],
                                         op0=ALU.mult, op1=ALU.add).then_inc(normed, 1)

            def oT_tile_lo_of(b, i):
                dve.wait_ge(oT_hi_done, b * NT + i + 1)
                dve.tensor_tensor(oT_tile_lo[:], oT[:, :, i * P:(i + 1) * P], oT_tile_hi[:].bitcast(F32),
                                  ALU.subtract).then_inc(oT_lo_done, 1)

            def gate(b, i):
                dve.wait_ge(y_done, b * NT + i + 1)
                if i == 0:
                    dve.wait_ge(ga_in, b * 16 + 16)
                if not (isinstance(b, int) and b == 0 and i == 0):
                    dve.wait_ge(x1_done, b * NT + i)
                dve.tensor_tensor(gated[:], mix_ps[:], row_ga[:], ALU.mult).then_inc(gated_done, 1)

            ln_stats(0, 0)
            for i in range(NT):
                ln_apply(0, i)
                if i + 1 < NT:
                    ln_stats(0, i + 1)
                hT_lo_of(0, i)
                if i > 0:
                    ropes(i - 1, i - 1)
                    v_low(i - 1, i - 1, 0)
                    rotate(i - 1, i - 1)
                if i > 1:
                    qk_lo(i - 2, i - 2, 0)
            ropes(NT - 1, NT - 1)
            v_low(NT - 1, NT - 1, 0)
            rotate(NT - 1, NT - 1)

            def body(b, kind, steps):
                for k in range(steps):
                    st = Step(b, k, kind)
                    i = st.i
                    todo = chunks_of(i)
                    if kind != "first":
                        for j in [j for j, s in enumerate(WO_STEP) if s + 1 == k]:
                            gate(b - 1, j)
                    if st.scores:
                        maxima(st)
                    if not (kind == "tail" and k > NT // 2):
                        pT_lo_of(st, todo[0])
                    for j in st.out:
                        oT_tile_lo_of(b - 1, j)
                    if st.natural:
                        ropes(st.n + NT - 1, (i - 1) % NT)
                        v_low(st.n + NT - 1, (i - 1) % NT, (st.h + (i > 0)) % 2)
                        rotate(st.n + NT - 1, (i - 1) % NT)
                    if st.scores:
                        inverse(st)
                        if i % GT == GT - 1:
                            normalise(st)
                    if st.ln(0) is not None:
                        hT_lo_of(b + 1, st.ln(0))
                    if st.turn:
                        qk_lo(st.n + NT - 2, (i - 2) % NT, (st.h + (i > 1)) % 2)
                    if len(todo) > 1 and not (kind == "tail" and k > NT // 2):
                        pT_lo_of(st, todo[1])
                    if st.ln(-1) is not None:
                        ln_apply(b + 1, st.ln(-1))
                    if st.ln(-2) is not None:
                        ln_stats(b + 1, st.ln(-2))

            batch_rows(dve, body)

        @block.gpsimd
        def _(pool):
            pool.memset(minus_half[:], -0.5).then_inc(half_set, 1)
            pool.wait_ge(half_set, 1)

            def normalise(st):
                i = st.i
                wait_alone(pool, inv_done, st.n + 1, half_set, 1)
                p = probs[:, p_column(i):p_column(i + 1)]
                pool.tensor_scalar(p, p, inv_sum[:, i:i + 1], None, ALU.mult).then_inc(probs_done, 1)

            def inverse_deviation(b, i):
                wait_alone(pool, mv_done, b * NT + i + 1, half_set, 1)
                pool.tensor_scalar(rstd[:, i % 2, :], mean_var[:, i % 2, 1:2], EPS, None, ALU.add).then_inc(eps_done, 1)
                pool.wait_ge(eps_done, b * NT + i + 1)
                pool.tensor_tensor(rstd[:, i % 2, :], rstd[:, i % 2, :], minus_half[:], ALU.pow).then_inc(rstd_done, 1)

            def residual(b, i):
                pool.wait_ge(gated_done, b * NT + i + 1)
                pool.wait_ge(x_res_in[i % 2], b * (NT // 2 * 16) + (i // 2 + 1) * 16)
                x = x_res[:, i % 2, :]
                pool.tensor_tensor(x, x, gated[:], ALU.add).then_inc(x1_done, 1)

            def w1_low(m):
                pool.wait_ge(w1_hi_made, m + 1)
                pool.tensor_tensor(w1_piece(w1["lo"], m), w1["stage"][:, m % W1_STAGES, :],
                                   w1_piece(w1["hi"], m).bitcast(F32), ALU.subtract).then_inc(w1_lo_made, 1)

            for i in range(NT):
                inverse_deviation(0, i)

            def body(b, kind, steps):
                for k in range(steps):
                    st = Step(b, k, kind)
                    i = st.i
                    if kind != "first":
                        for j in [j for j, s in enumerate(WO_STEP) if s + 1 == k]:
                            residual(b - 1, j)
                    if st.scores and i % GT < GT - 1:
                        normalise(st)
                    t_ln = st.ln(-2)
                    if t_ln is not None:
                        inverse_deviation(b + 1, t_ln)
                    for m in st.w1_pieces(W1_SPLIT):
                        w1_low(m)

            batch_rows(pool, body)


def ffn(nc, t, mod_table, x1, out, w1, hT_hi, ident):
    x1_groups = x1.rearrange("b (g i p) d -> b g p i d", p=P, i=GT)
    out_groups = out.rearrange("b (g i p) d -> b g p i d", p=P, i=GT)
    N = GT * P
    LN_SLOT = [7, 9, 11, 13]

    with ExitStack() as ctx:
        def sb(name, shape, dt=F32):
            return ctx.enter_context(nc.sbuf_tensor(name, shape, dt))

        def psum(name):
            return ctx.enter_context(nc.psum_tensor(name, [P, 512], F32))

        def sem(name):
            return ctx.enter_context(nc.semaphore(name))

        w1_hi, w1_lo = w1["hi"], w1["lo"]
        w2_hi = sb("w2_hi", [P, IB, D], F32R)
        w2_lo = sb("w2_lo", [P, IB, D], F32R)
        x = sb("x1_group", [P, 2, GT, D])
        xn = sb("x1_normed", [P, 2, D])
        hT_lo = sb("h2T_lo", [P, 2, KB, N], F32R)
        relu = sb("relu", [P, 2, N])
        aT_hi = sb("aT_hi", [P, 2, N], F32R)
        aT_lo = sb("aT_lo", [P, 2, N], F32R)
        gated = sb("z_gated", [P, 2, D])
        row_cb = sb("row_cb", [P, D])
        row_sb = sb("row_sb", [P, D])
        row_gb = sb("row_gb", [P, D])
        row_b2g = sb("row_b2g", [P, D])
        b1_cols = sb("b1_cols", [P, IB])
        stats = sb("stats2", [P, 2, 6])
        mean_var = sb("mean_var2", [P, 2, 2])
        rstd = sb("rstd2", [P, 2, 1])
        minus_half = sb("minus_half2", [P, 1])

        a_ps = [psum(f"a_ps{j}") for j in range(2)]
        z_ps = [psum(f"z_ps{j}") for j in range(GT)]
        ln_ps = psum("ln_ps")

        const_in = sem("ffn_tables_loaded")
        w2_in = [sem(f"w2_stage{j}_loaded") for j in range(2)]
        w2_hi_made = sem("w2_hi_made")
        w2_made = sem("w2_split")
        x_in = [sem(f"x1_{j}_loaded") for j in range(2)]
        out_done = [sem(f"out_{j}_stored") for j in range(2)]
        ln_rows_in = sem("ffn_ln_rows_loaded")
        gb_in = sem("gb_loaded")
        bn_done = sem("ffn_bn_done")
        mv_done = sem("ffn_mean_var_done")
        scaled = sem("ffn_x_scaled")
        normed = sem("ffn_x_normed")
        half_set = sem("ffn_minus_half_set")
        eps_done = sem("ffn_eps_added")
        rstd_done = sem("ffn_rstd_done")
        ln_turned = sem("ffn_ln_turned")
        hT_hi_done = sem("h2T_hi_done")
        hT_lo_done = sem("h2T_lo_done")
        a_done = sem("a_done")
        relu_done = sem("relu_done")
        a_lo_done = sem("a_lo_done")
        up_used = sem("aT_used")
        z_done = sem("z_done")
        z_out = sem("z_gated_done")
        biased = sem("residual_biased")
        summed = sem("out_summed")

        PIECE = GT // 2
        PIECES = IB // PIECE
        W2_SPLIT = [[2], [3], [4, 5], [6, 7]]
        w2_blocks = t["W2"].rearrange("(q i p) d -> q p i d", p=P, i=PIECE)

        def stage(m):
            return x[:, 1, m % 2 * PIECE:(m % 2 + 1) * PIECE, :]

        block = ctx.enter_context(nc.Block())

        def groups(engine, body):
            body(0, 0, "first")
            body(0, 1, "middle")
            with engine.Fori(1, B - 1) as b:
                body(b, 0, "middle")
                body(b, 1, "middle")
            body(B - 1, 0, "middle")
            body(B - 1, 1, "last")

        def after(b, g):
            return (b, 1) if g == 0 else (b + 1, 0)

        def tiles(b, g):
            return b * (GROUPS * GT) + g * GT

        @block.sync
        def _(sp):
            def load_group(b, g):
                if not (isinstance(b, int) and b == 0):
                    sp.wait_ge(out_done[g], b * 16)
                sp.dma_start(x[:, g, :, :], x1_groups[b, g]).then_inc(x_in[g], 16)

            def load_ln_rows(b):
                if not (isinstance(b, int) and b == 0):
                    sp.wait_ge(normed, b * (GROUPS * GT))
                    sp.wait_ge(biased, b * (GROUPS * GT))
                for r, row in ((CB, row_cb), (SB, row_sb), (B2G, row_b2g)):
                    sp.dma_start(row[:], mod_table[b, r, :].partition_broadcast(P)).then_inc(ln_rows_in, 16)

            def load_gb(b):
                if not (isinstance(b, int) and b == 0):
                    sp.wait_ge(z_out, b * (GROUPS * GT))
                sp.dma_start(row_gb[:], mod_table[b, GB, :].partition_broadcast(P)).then_inc(gb_in, 16)

            def store(b, g):
                wait_alone(sp, summed, tiles(b, g) + GT, gb_in, 16)
                sp.dma_start(out_groups[b, g], x[:, g, :, :]).then_inc(out_done[g], 16)

            load_group(0, 0)
            load_ln_rows(0)
            sp.dma_start(b1_cols[:], t["b1"].rearrange("(i p) -> p i", p=P),
                         allow_slow_non_contiguous=True).then_inc(const_in, 16)
            for m in range(PIECES):
                if m >= 2:
                    sp.wait_ge(w2_made, m - 1)
                sp.dma_start(stage(m), w2_blocks[m]).then_inc(w2_in[m % 2], 16)
            load_gb(0)
            sp.wait_ge(w2_made, PIECES)
            load_group(0, 1)

            def body(b, g, kind):
                if kind != "first":
                    pb, pg = (b, 0) if g == 1 else (b - 1, 1)
                    store(pb, pg)
                    if g == 0:
                        load_gb(b)
                        load_group(b, 1)
                    elif not (isinstance(b, int) and b == B - 1):
                        load_group(b + 1, 0)
                if g == 0 and not (isinstance(b, int) and b == B - 1):
                    load_ln_rows(b + 1)
            groups(sp, body)
            store(B - 1, 1)
            for j in range(2):
                sp.wait_ge(out_done[j], 16 * B)

        @block.tensor
        def _(pe):
            def three(out_ps, a_hi, a_lo, b_hi, b_lo, start, stop):
                pe.matmul(out_ps, a_hi, b_hi, start=start, stop=False)
                pe.matmul(out_ps, a_hi, b_lo, start=False, stop=False)
                return pe.matmul(out_ps, a_lo, b_hi, start=False, stop=stop)

            def turn(b, g, j):
                n = tiles(b, g) + j
                pe.wait_ge(normed, n + 1)
                if not (isinstance(n, int) and n == 0):
                    pe.wait_ge(hT_lo_done, n)
                for kb in range(KB):
                    ins = pe.transpose(ln_ps[:, kb * P:(kb + 1) * P], xn[:, j % 2, kb * P:(kb + 1) * P], ident[:])
                ins.then_inc(ln_turned, 1)

            def up(b, g, i):
                n = b * (GROUPS * IB) + g * IB + i
                if i == 0:
                    pe.wait_ge(hT_lo_done, tiles(b, g) + GT)
                if not (isinstance(n, int) and n < 2):
                    pe.wait_ge(relu_done, n - 1)
                for kb in range(KB):
                    ins = three(a_ps[i % 2][:], w1_hi[:, kb, i * P:(i + 1) * P], w1_lo[:, kb, i * P:(i + 1) * P],
                                hT_hi[:, g, kb, :], hT_lo[:, g, kb, :], kb == 0, kb == KB - 1)
                ins.then_inc(a_done, 1)

            def down(b, g, i):
                n = b * (GROUPS * IB) + g * IB + i
                pe.wait_ge(a_lo_done, n + 1)
                for j in range(GT):
                    if i == 0 and not (isinstance(b, int) and b == 0 and g == 0):
                        pe.wait_ge(z_out, tiles(b, g) - GT + j + 1)
                    cols = slice(j * P, (j + 1) * P)
                    ins = three(z_ps[j][:], aT_hi[:, i % 2, cols], aT_lo[:, i % 2, cols],
                                w2_hi[:, i, :], w2_lo[:, i, :], i == 0, i == IB - 1)
                    if i == IB - 1:
                        ins.then_inc(z_done, 1)
                if i < IB - 1:
                    ins.then_inc(up_used, 1)

            for j in range(GT):
                turn(0, 0, j)

            def body(b, g, kind):
                for i in range(IB):
                    up(b, g, i)
                    if i > 0:
                        if kind == "first":
                            pe.wait_ge(w2_made, (i - 1) // PIECE + 1)
                        down(b, g, i - 1)
                    elif kind != "first":
                        pb, pg = (b, 0) if g == 1 else (b - 1, 1)
                        down(pb, pg, IB - 1)
                    if i in LN_SLOT and kind != "last":
                        turn(*after(b, g), LN_SLOT.index(i))

            groups(pe, body)
            down(B - 1, 1, IB - 1)

        @block.scalar
        def _(act):
            def hT_hi_of(b, g, j):
                act.wait_ge(ln_turned, tiles(b, g) + j + 1)
                act.activation(hT_hi[:, g, :, j * P:(j + 1) * P], ln_ps[:].rearrange("p (k c) -> p k c", k=KB),
                               ACT.Copy).then_inc(hT_hi_done, 1)

            def activate(b, g, i):
                n = b * (GROUPS * IB) + g * IB + i
                act.wait_ge(a_done, n + 1)
                if not (isinstance(n, int) and n < 2):
                    act.wait_ge(a_lo_done, n - 1)
                act.activation(relu[:, i % 2, :], a_ps[i % 2][:], ACT.Relu, bias=b1_cols[:, i:i + 1])
                act.activation(aT_hi[:, i % 2, :], a_ps[i % 2][:], ACT.Relu,
                               bias=b1_cols[:, i:i + 1]).then_inc(relu_done, 1)

            def w2_high(m):
                act.wait_ge(w2_in[m % 2], 16 * (m // 2 + 1))
                act.activation(w2_hi[:, m * PIECE:(m + 1) * PIECE, :], stage(m), ACT.Copy).then_inc(w2_hi_made, 1)

            for j in range(GT):
                hT_hi_of(0, 0, j)
            for m in range(2):
                w2_high(m)
            act.wait_ge(const_in, 16)

            def body(b, g, kind):
                for i in range(IB):
                    activate(b, g, i)
                    if kind == "first" and i < len(W2_SPLIT):
                        for m in W2_SPLIT[i]:
                            w2_high(m)
                    if i in LN_SLOT and kind != "last":
                        hT_hi_of(*after(b, g), LN_SLOT.index(i))
            groups(act, body)

        @block.vector
        def _(dve):
            def w2_low(m):
                blocks = slice(m * PIECE, (m + 1) * PIECE)
                dve.wait_ge(w2_hi_made, m + 1)
                dve.tensor_tensor(w2_lo[:, blocks, :], stage(m), w2_hi[:, blocks, :].bitcast(F32),
                                  ALU.subtract).then_inc(w2_made, 1)

            def ln_stats(b, g, j):
                n = tiles(b, g) + j
                if j == 0:
                    dve.wait_ge(x_in[g], b * 16 + 16)
                dve.bn_stats(stats[:, j % 2, :], x[:, g, j, :]).then_inc(bn_done, 1)
                wait_alone(dve, bn_done, n + 1, bn_done, 1)
                dve.bn_aggr(mean_var[:, j % 2, :], stats[:, j % 2, :]).then_inc(mv_done, 1)

            def ln_apply(b, g, j):
                n = tiles(b, g) + j
                if j == 0 and g == 0:
                    dve.wait_ge(ln_rows_in, b * 48 + 48)
                dve.wait_ge(mv_done, n + 1)
                if not (isinstance(n, int) and n < 2):
                    dve.wait_ge(ln_turned, n - 1)
                dve.scalar_tensor_tensor(out=xn[:, j % 2, :], in0=x[:, g, j, :], scalar=mean_var[:, j % 2, 0:1],
                                         in1=row_cb[:], op0=ALU.subtract, op1=ALU.mult).then_inc(scaled, 1)
                dve.wait_ge(scaled, n + 1)
                dve.wait_ge(rstd_done, n + 1)
                dve.scalar_tensor_tensor(out=xn[:, j % 2, :], in0=xn[:, j % 2, :], scalar=rstd[:, j % 2, :],
                                         in1=row_sb[:], op0=ALU.mult, op1=ALU.add).then_inc(normed, 1)

            def hT_lo_of(b, g, j):
                cols = slice(j * P, (j + 1) * P)
                dve.wait_ge(hT_hi_done, tiles(b, g) + j + 1)
                dve.tensor_tensor(hT_lo[:, g, :, cols], ln_ps[:].rearrange("p (k c) -> p k c", k=KB),
                                  hT_hi[:, g, :, cols].bitcast(F32), ALU.subtract).then_inc(hT_lo_done, 1)

            def a_low(b, g, i):
                n = b * (GROUPS * IB) + g * IB + i
                dve.wait_ge(relu_done, n + 1)
                dve.tensor_tensor(aT_lo[:, i % 2, :], relu[:, i % 2, :], aT_hi[:, i % 2, :].bitcast(F32),
                                  ALU.subtract).then_inc(a_lo_done, 1)

            def gate(b, g, j):
                n = tiles(b, g) + j
                dve.wait_ge(z_done, n + 1)
                if j == 0 and g == 0:
                    dve.wait_ge(gb_in, b * 16 + 16)
                if not (isinstance(n, int) and n < 2):
                    dve.wait_ge(summed, n - 1)
                dve.tensor_tensor(gated[:, j % 2, :], z_ps[j][:], row_gb[:], ALU.mult).then_inc(z_out, 1)

            ln_stats(0, 0, 0)
            for j in range(GT):
                ln_apply(0, 0, j)
                if j + 1 < GT:
                    ln_stats(0, 0, j + 1)
                hT_lo_of(0, 0, j)
            for m in range(2):
                w2_low(m)

            def body(b, g, kind):
                for i in range(IB):
                    a_low(b, g, i)
                    if kind == "first" and i < len(W2_SPLIT):
                        for m in W2_SPLIT[i]:
                            w2_low(m)
                    if i == 0 and kind != "first":
                        pb, pg = (b, 0) if g == 1 else (b - 1, 1)
                        for j in range(GT):
                            gate(pb, pg, j)
                    if kind != "last":
                        if i + 2 in LN_SLOT:
                            ln_stats(*after(b, g), LN_SLOT.index(i + 2))
                        if i + 1 in LN_SLOT:
                            ln_apply(*after(b, g), LN_SLOT.index(i + 1))
                        if i in LN_SLOT:
                            hT_lo_of(*after(b, g), LN_SLOT.index(i))
            groups(dve, body)
            for j in range(GT):
                gate(B - 1, 1, j)

        @block.gpsimd
        def _(pool):
            pool.memset(minus_half[:], -0.5).then_inc(half_set, 1)
            pool.wait_ge(half_set, 1)

            def inverse_deviation(b, g, j):
                n = tiles(b, g) + j
                wait_alone(pool, mv_done, n + 1, half_set, 1)
                pool.tensor_scalar(rstd[:, j % 2, :], mean_var[:, j % 2, 1:2], EPS, None, ALU.add).then_inc(eps_done, 1)
                pool.wait_ge(eps_done, n + 1)
                pool.tensor_tensor(rstd[:, j % 2, :], rstd[:, j % 2, :], minus_half[:], ALU.pow).then_inc(rstd_done, 1)

            def bias(b, g, j):
                pool.wait_ge(normed, tiles(b, g) + j + 1)
                pool.tensor_tensor(x[:, g, j, :], x[:, g, j, :], row_b2g[:], ALU.add).then_inc(biased, 1)

            def residual(b, g, j):
                n = tiles(b, g) + j
                pool.wait_ge(z_out, n + 1)
                pool.wait_ge(biased, n + 1)
                pool.tensor_tensor(x[:, g, j, :], x[:, g, j, :], gated[:, j % 2, :], ALU.add).then_inc(summed, 1)

            for j in range(GT):
                inverse_deviation(0, 0, j)
                bias(0, 0, j)

            def body(b, g, kind):
                if kind != "first":
                    pb, pg = (b, 0) if g == 1 else (b - 1, 1)
                    for j in range(GT):
                        residual(pb, pg, j)
                if kind != "last":
                    for j in range(GT):
                        inverse_deviation(*after(b, g), j)
                        bias(*after(b, g), j)
            groups(pool, body)
            for j in range(GT):
                residual(B - 1, 1, j)


def build(nc, t, out):
    mod_table = nc.dram_tensor("mod_table", [B, 7, D], F32, kind="Internal").ap()
    x1 = nc.dram_tensor("x1", [B, T, D], F32, kind="Internal").ap()
    with ExitStack() as outer:
        word, qkv_size, hT_size, w1_size = 4, KB * H * QKV, KB * T, KB * INTER
        start = (nc.sbuf_base + 31) // 32 * 32
        outer.enter_context(nc.sbuf_tensor("region", [P, 2 * qkv_size + 2 * hT_size], F32))
        ident = outer.enter_context(nc.sbuf_tensor("ident", [P, P], F32))
        behind_w1 = 2 * w1_size
        assert behind_w1 == 2 * qkv_size + hT_size

        def placed(name, at, shape, dt=F32R):
            return nc.alloc_sbuf_tensor_at(name, shape, dt, offset=start + word * at)

        w1 = {
            "hi": placed("w1_hi", 0, [P, KB, INTER]),
            "lo": placed("w1_lo", w1_size, [P, KB, INTER]),
            "stage": placed("w1_stage", behind_w1, [P, W1_STAGES, W1_PIECE], F32),
        }
        with ExitStack() as ctx:
            def sb(name, shape, dt=F32):
                return ctx.enter_context(nc.sbuf_tensor(name, shape, dt))

            w = {
                "wqkv_hi": placed("wqkv_hi", 0, [P, KB, H, QKV]),
                "wqkv_lo": placed("wqkv_lo", qkv_size, [P, KB, H, QKV]),
                "hT_hi": placed("hT_hi", 2 * qkv_size, [P, KB, T]),
                "hT_lo": placed("hT_lo", behind_w1, [P, KB, T]),
                "wo_hi": sb("wo_hi", [P, H, D], F32R), "wo_lo": sb("wo_lo", [P, H, D], F32R),
                "cos": sb("cos", [P, NT, ROT]), "sin": sb("sin", [P, NT, ROT]), "ident": ident,
                "ident16": sb("ident16", [P, P], BF16), "mask16": sb("mask16", [P, P], BF16),
            }
            prepare(nc, t, mod_table, w)
            attention(nc, t, mod_table, x1, w, w1)
        hT_hi = placed("h2T_hi", behind_w1, [P, GROUPS, KB, GT * P])
        ffn(nc, t, mod_table, x1, out, w1, hT_hi, ident)


def tables():
    freqs = np.power(np.float32(10000.0), -np.arange(HALF, dtype=np.float32) / np.float32(HALF)).astype(np.float32)
    radians = np.arange(T, dtype=np.float32)[:, None] * freqs[None, :]
    cos, sin = np.cos(radians).astype(np.float32), np.sin(radians).astype(np.float32)
    by_tile = lambda a: np.ascontiguousarray(a.reshape(NT, P, ROT).transpose(1, 0, 2))
    upper = np.triu(np.ones((P, P), np.float32), 1)
    return {
        "cos": by_tile(np.concatenate([cos, cos], 1)), "sin": by_tile(np.concatenate([-sin, sin], 1)), "ident": np.eye(P, dtype=np.float32),
        "mask": upper * np.float32(MASKED),
    }


_NAMES = {"L0_attn_x": "x", "L0_attn_wq": "wq", "L0_attn_wk": "wk", "L0_attn_wv": "wv", "L0_attn_wo": "wo",
          "L0_ffn_W1": "W1", "L0_ffn_b1": "b1", "L0_ffn_W2": "W2", "L0_ffn_b2": "b2", "L0_c": "c", "L0_wmod": "wmod"}


def kernel(**inputs):
    import concourse.bacc as bacc
    from concourse.bass_utils import run_bass_kernel_spmd

    nc = bacc.Bacc("TRN2", target_bir_lowering=False, num_devices=1)
    arrays, t = {}, {}
    named = {short: np.ascontiguousarray(inputs[name]) for name, short in _NAMES.items()}
    for short, a in {**named, **tables()}.items():
        arrays[f"in_{short}"] = a
        t[short] = nc.dram_tensor(f"in_{short}", a.shape, mybir.dt.from_np(a.dtype), kind="ExternalInput").ap()
    out = nc.dram_tensor("out", (B, T, D), F32, kind="ExternalOutput").ap()
    build(nc, t, out)
    r = run_bass_kernel_spmd(nc, [arrays], core_ids=[0])
    return r.results[0]["out"]
```

```python
from contextlib import ExitStack

import numpy as np

import concourse.bass as bass
from concourse import mybir

F32 = mybir.dt.float32
F32R = mybir.dt.float32r
BF16 = mybir.dt.bfloat16
ALU = mybir.AluOpType
ACT = mybir.ActivationFunctionType
AX = mybir.AxisListType

P = 128
B, T, D = 8, 1024, 512
H, DH = 4, 128
INTER = 2048
KB = D // P
NT = T // P
IB = INTER // P
ROT = DH // 2
HALF = ROT // 2
QKV = 3 * DH
EPS = 1e-5
GATE_MIN = 0.25
MASKED = -1e30
STEPS = H * NT
CHUNKS = NT + NT // 2
GT = 4
GROUPS = NT // GT
SA, CA, GA, SB, CB, GB, B2G = range(7)
WO_STEP = [1, 2, 4, 5, 7, 8, 10, 11]
WO_TAIL = [1, 2, 3, 4, 5, 6, 7, 8]
LN_STEP = [17, 19, 21, 23, 25, 26, 28, 30]
TAIL_STEPS = 10
X_EARLY = 2
W1_PIECE = 1024
W1_STAGES = KB * T // W1_PIECE
W1_LOAD = {"last": [24, 24, 24, 24, 27, 29, 31], "tail": [2]}
W1_SPLIT = {"last": [25, 27, 29, 31], "tail": [1, 3, 5, 7]}


def p_column(i):
    return P * (i * (i + 1) // 2)


def chunks_of(i):
    return [2 * i, 2 * i + 1] if i < NT // 2 else [NT // 2 + i]


class Step:

    def __init__(self, b, k, kind):
        self.b, self.k, self.kind = b, k, kind
        self.h, self.i = divmod(k, NT)
        self.n = b * STEPS + k
        self.scores = kind != "tail"
        self.project = self.has_project(k)
        self.natural = (kind not in ("first", "tail")) if k == 0 else self.has_project(k - 1)
        self.turn = kind != "tail" if k < 2 else self.has_project(k - 2)
        wo_step = {"first": [], "tail": WO_TAIL}.get(kind, WO_STEP)
        self.out = [j for j, s in enumerate(wo_step) if s == k]
        self.gate = [j for j, s in enumerate(wo_step) if s + 1 == k]

    def has_project(self, k):
        return self.kind in ("first", "middle") or (self.kind == "last" and k < STEPS - NT)

    def has_chunk(self, s):
        if s < NT:
            return not (self.kind == "first" and self.h == 0 or self.kind == "tail" and self.h > 0)
        return self.kind != "tail"

    def chunk_count(self, s):
        return self.b * (H * CHUNKS) + self.h * CHUNKS + s + 1 - NT

    def chunk(self, s):
        if s < 0:
            return 0, GT - 1, (self.h + 1) % 2
        if s < NT:
            return 1, s, (self.h + 1) % 2
        return 0, s - NT, self.h % 2

    def w1_pieces(self, schedule):
        before = 0 if self.kind == "last" else len(schedule["last"])
        return [before + m for m, k in enumerate(schedule.get(self.kind, [])) if k == self.k]

    def ln(self, step):
        known = self.kind in ("first", "middle") and self.k - step in LN_STEP
        return LN_STEP.index(self.k - step) if known else None


def batch_rows(engine, body):
    body(0, "first", STEPS)
    with engine.Fori(1, B - 1) as b:
        body(b, "middle", STEPS)
    body(B - 1, "last", STEPS)
    body(B, "tail", TAIL_STEPS)


def wait_alone(engine, semaphore, value, passed, at_least):
    value = value if isinstance(value, int) else engine.to_reg(value)
    engine.wait_ge(passed, at_least)
    engine.wait_ge(semaphore, value)


def prepare(nc, t, mod_table, w):
    with ExitStack() as ctx:
        def sb(name, shape, dt=F32):
            return ctx.enter_context(nc.sbuf_tensor(name, shape, dt))

        def sem(name):
            return ctx.enter_context(nc.semaphore(name))

        stage = w["stage"]
        wmod = sb("wmod_stage", [P, KB, 6 * D])
        mask = sb("mask", [P, P])
        c_cols = sb("c_cols", [P, KB, B])
        e_cols = sb("e_cols", [P, KB, B])
        d_cols = sb("d_cols", [P, KB, B])
        r_cols = sb("r_cols", [P, KB, B])
        silu = sb("silu", [P, KB, B])
        rows = sb("mod_rows", [B, 7, D])
        b2_rows = sb("b2_rows", [B, D])
        mag = sb("gate_magnitude", [B, 2, D])
        sign = sb("gate_sign", [B, 2, D])
        acc = [ctx.enter_context(nc.psum_tensor(f"mod_acc{r}", [P, D], F32)) for r in range(6)]

        c_in = sem("c_loaded")
        small_in = sem("ident_mask_b2_loaded")
        tables_in = sem("rope_tables_x_loaded")
        wmod_in = [[sem(f"wmod{k}_half{half}_loaded") for half in range(2)] for k in range(KB)]
        stage_in = [sem(f"stage{j}_loaded") for j in range(3)]
        hi_made = sem("weight_hi_made")
        exp_done = sem("exp_done")
        chain = sem("vector_chain")
        silu_done = sem("silu_done")
        acc_done = sem("mod_rows_multiplied")
        magnitude_done = sem("gate_magnitude_done")
        plain_done = sem("shift_scale_rows_done")
        rows_done = sem("mod_rows_done")
        first_stored = sem("ca_sa_rows_stored")
        stored = sem("other_mod_rows_stored")
        finish = [GA, GB, CA, SA, CB, SB]

        block = ctx.enter_context(nc.Block())

        def parts(j, kb):
            cols = slice(j * DH, (j + 1) * DH)
            return w["wqkv_hi"][:, kb, :, cols], w["wqkv_lo"][:, kb, :, cols], 1.0 / DH if j == 0 else 1.0

        @block.sync
        def _(sp):
            for kb in range(KB):
                sp.dma_start(c_cols[:, kb, :], t["c"][:, kb * P:(kb + 1) * P].rearrange("b p -> p b"),
                             allow_slow_non_contiguous=True).then_inc(c_in, 16)
            for k in range(KB):
                for half in range(2):
                    cols = slice(half * 3 * D, (half + 1) * 3 * D)
                    sp.dma_start(wmod[:, k, cols], t["wmod"][k * P:(k + 1) * P, cols]).then_inc(wmod_in[k][half], 16)
            sp.dma_start(b2_rows[:], t["b2"].rearrange("(a d) -> a d", a=1).to_broadcast([B, D])).then_inc(small_in, 16)
            sp.dma_start(w["ident"][:], t["ident"]).then_inc(small_in, 16)
            sp.dma_start(mask[:], t["mask"]).then_inc(small_in, 16)
            for j, name in enumerate(("wq", "wk", "wv")):
                for kb in range(KB):
                    sp.dma_start(stage[:, j, kb, :, :],
                                 t[name][:, kb * P:(kb + 1) * P, :].rearrange("h p k -> p h k")).then_inc(stage_in[j], 16)
            sp.dma_start(w["cos"][:], t["cos"]).then_inc(tables_in, 16)
            sp.dma_start(w["sin"][:], t["sin"]).then_inc(tables_in, 16)
            sp.dma_start(w["probs"][:, 0:X_EARLY * D].rearrange("p (i d) -> p i d", i=X_EARLY),
                         t["x"][0, 0:X_EARLY * P, :].rearrange("(i p) d -> p i d", p=P)).then_inc(tables_in, 16)
            sp.wait_ge(plain_done, 2)
            sp.dma_start(mod_table[:, SA:CA + 1, :], rows[:, SA:CA + 1, :]).then_inc(first_stored, 16)
            sp.wait_ge(first_stored, 16)
            sp.dma_start(w["row_ca"][:], mod_table[0, CA, :].partition_broadcast(P)).then_inc(tables_in, 16)
            sp.dma_start(w["row_sa"][:], mod_table[0, SA, :].partition_broadcast(P)).then_inc(tables_in, 16)
            sp.wait_ge(plain_done, 4)
            sp.wait_ge(rows_done, 1)
            sp.dma_start(mod_table[:, GA:B2G + 1, :], rows[:, GA:B2G + 1, :]).then_inc(stored, 16)
            sp.wait_ge(tables_in, 80)
            sp.wait_ge(stored, 16)

        @block.scalar
        def _(act):
            def weights_high(j):
                act.wait_ge(stage_in[j], 16 * KB)
                for kb in range(KB):
                    hi, _, factor = parts(j, kb)
                    act.activation(hi, stage[:, j, kb, :, :], ACT.Copy, scale=factor).then_inc(hi_made, 1)

            act.wait_ge(c_in, 16 * KB)
            act.activation(e_cols[:], c_cols[:], ACT.Exp, scale=-1.0).then_inc(exp_done, 1)
            weights_high(0)
            weights_high(1)
            for j, r in enumerate((GA, GB)):
                act.wait_ge(acc_done, finish.index(r) + 1)
                act.activation(mag[:, j, :], acc[r][0:B, :], ACT.Abs).then_inc(magnitude_done, 1)
            for r in (CA, SA, CB, SB):
                act.wait_ge(acc_done, finish.index(r) + 1)
                act.activation(rows[:, r, :], acc[r][0:B, :], ACT.Identity,
                               bias=1.0 if r in (CA, CB) else 0.0).then_inc(plain_done, 1)
            weights_high(2)

        @block.vector
        def _(dve):
            n = [0]

            def link(ins):
                n[0] += 1
                ins.then_inc(chain, 1)
                dve.wait_ge(chain, n[0])

            def weights_low(j, kbs=range(KB)):
                for kb in kbs:
                    hi, lo, factor = parts(j, kb)
                    dve.wait_ge(hi_made, j * KB + kb + 1)
                    dve.scalar_tensor_tensor(out=lo, in0=stage[:, j, kb, :, :], scalar=factor,
                                             in1=hi.bitcast(F32), op0=ALU.mult, op1=ALU.subtract)

            dve.wait_ge(exp_done, 1)
            link(dve.tensor_scalar(d_cols[:], e_cols[:], 1.0, None, ALU.add))
            link(dve.reciprocal(r_cols[:], d_cols[:]))
            dve.tensor_tensor(silu[:], c_cols[:], r_cols[:], ALU.mult).then_inc(silu_done, 1)
            weights_low(0)
            dve.wait_ge(small_in, 16 * 3)
            dve.tensor_copy(w["ident16"][:], w["ident"][:])
            dve.tensor_copy(w["mask16"][:], mask[:])
            weights_low(1)
            for j, r in enumerate((GA, GB)):
                dve.wait_ge(magnitude_done, j + 1)
                dve.tensor_scalar(sign[:, j, :], acc[r][0:B, :], 0.0, 2.0, ALU.is_ge, ALU.mult)
                link(dve.tensor_scalar(mag[:, j, :], mag[:, j, :], GATE_MIN, None, ALU.max))
                link(dve.scalar_tensor_tensor(out=rows[:, r, :], in0=sign[:, j, :], scalar=-1.0,
                                              in1=mag[:, j, :], op0=ALU.add, op1=ALU.mult))
            dve.tensor_tensor(rows[:, B2G, :], rows[:, GB, :], b2_rows[:], ALU.mult).then_inc(rows_done, 1)
            weights_low(2, range(KB // 2, KB))

        @block.gpsimd
        def _(pool):
            for kb in range(KB // 2):
                hi, lo, _ = parts(2, kb)
                pool.wait_ge(hi_made, 2 * KB + kb + 1)
                pool.tensor_tensor(lo, stage[:, 2, kb, :, :], hi.bitcast(F32), ALU.subtract)

        @block.tensor
        def _(pe):
            pe.wait_ge(silu_done, 1)
            for k in range(KB):
                order = range(6) if k == 0 else finish
                for r in order:
                    if r == order[0]:
                        pe.wait_ge(wmod_in[k][r // 3], 16)
                    elif r == order[3 if k == 0 else 1]:
                        pe.wait_ge(wmod_in[k][r // 3], 16)
                    ins = pe.matmul(acc[r][0:B, :], silu[:, k, :], wmod[:, k, r * D:(r + 1) * D],
                                    start=(k == 0), stop=(k == KB - 1))
                    if k == KB - 1:
                        ins.then_inc(acc_done, 1)


def attention(nc, t, mod_table, x1, w, w1, x_last_out):
    x_tiles = t["x"].rearrange("b (i p) d -> b i p d", p=P)
    x1_tiles = x1.rearrange("b (i p) d -> b i p d", p=P)

    with ExitStack() as ctx:
        def sb(name, shape, dt=F32):
            return ctx.enter_context(nc.sbuf_tensor(name, shape, dt))

        def psum(name, shape):
            return ctx.enter_context(nc.psum_tensor(name, shape, F32))

        def sem(name):
            return ctx.enter_context(nc.semaphore(name))

        def pair(name, shape):
            return sb(name + "_hi", shape, F32R), sb(name + "_lo", shape, F32R)

        wqkv_hi, wqkv_lo, wo_hi, wo_lo = w["wqkv_hi"], w["wqkv_lo"], w["wo_hi"], w["wo_lo"]
        ident = w["ident"]
        hT_hi, hT_lo = w["hT_hi"], w["hT_lo"]
        qT_hi, qT_lo = pair("qT", [P, T])
        kT_hi, kT_lo = pair("kT", [P, 2, T])
        v_hi, v_lo = pair("v", [P, 2, NT, DH])
        pT_hi, pT_lo = pair("pT", [P, 2, GT * P])
        oT_tile_hi, oT_tile_lo = pair("oT_tile", [P, H, P])
        probs = w["probs"]
        oT = sb("oT", [P, H, T])
        x_ln = sb("x_ln", [P, 2, D])
        x_res = sb("x_res", [P, 2, D])
        gated = sb("gated", [P, D])
        nat = sb("qkv_natural", [P, 2, QKV])
        by_cos = sb("by_cos", [P, 2, ROT])
        by_sin = sb("by_sin", [P, 2, ROT])
        row_ca, row_sa = w["row_ca"], w["row_sa"]
        row_ga = sb("row_ga", [P, D])
        stats = sb("stats", [P, 2, 6])
        mean_var = sb("mean_var", [P, 2, 2])
        rstd = sb("rstd", [P, 2, 1])
        minus_half = sb("minus_half", [P, 1])
        neg_max = sb("neg_max", [P, NT])
        row_sum = sb("row_sum", [P, NT])
        inv_sum = sb("inv_sum", [P, NT])

        s_ps = psum("scores_ps", [P, T])
        qkv_ps = psum("qkv_ps", [P, 512])
        turn_ps = psum("turn_ps", [P, 512])
        pT_ps = [psum(f"pT_ps{j}", [P, GT * P]) for j in range(2)]
        o_ps = psum("o_ps", [P, GT * P])
        mix_ps = psum("mix_ps", [P, D])

        scores_done = sem("scores_done")
        qkv_done = sem("qkv_done")
        turned = sem("qk_turned")
        pT_done = sem("pT_done")
        pv_done = sem("pv_done")
        ln_turned = sem("ln_turned")
        y_done = sem("y_done")
        nat_copied = sem("nat_copied")
        exp_done = sem("exp_done")
        qk_hi_done = sem("qk_hi_done")
        pT_hi_done = sem("pT_hi_done")
        oT_done = sem("oT_done")
        hT_hi_done = sem("hT_hi_done")
        ropes_done = sem("ropes_done")
        v_lo_done = sem("v_lo_done")
        max_done = sem("max_done")
        inv_done = sem("inv_done")
        qk_lo_done = sem("qk_lo_done")
        pT_lo_done = sem("pT_lo_done")
        hT_lo_done = sem("hT_lo_done")
        bn_done = sem("bn_done")
        mv_done = sem("mean_var_done")
        scaled = sem("x_scaled")
        normed = sem("x_normed")
        gated_done = sem("gated_done")
        half_set = sem("minus_half_set")
        rotated = sem("rotated")
        v_hi_done = sem("v_hi_done")
        probs_done = sem("probs_normalised")
        last_probs_done = sem("last_probs_normalised")
        rest_probs_done = sem("rest_of_last_probs_normalised")
        eps_done = sem("eps_added")
        rstd_done = sem("rstd_done")
        oT_hi_done = sem("oT_tile_hi_done")
        oT_lo_done = sem("oT_tile_lo_done")
        x1_done = sem("x1_done")
        x_first_in = {i: sem(f"x_first{i}_loaded") for i in range(X_EARLY, NT)}
        wo_in = sem("wo_loaded")
        wo_hi_made = sem("wo_hi_made")
        wo_lo_made = sem("wo_lo_made")
        x_ln_in = [sem(f"x_ln{j}_loaded") for j in range(2)]
        x_res_in = [sem(f"x_res{j}_loaded") for j in range(2)]
        x_last_in = [sem(f"x_last{j}_loaded") for j in range(NT)]
        x1_out = [sem(f"x1_{j}_stored") for j in range(2)]
        w1_in = [sem(f"w1_stage{j}_loaded") for j in range(W1_STAGES)]
        w1_hi_made = sem("w1_hi_made")
        w1_lo_made = sem("w1_lo_made")
        ln_rows_in = sem("ln_rows_loaded")
        ga_in = sem("ga_loaded")

        def ln_tile(b, i):
            if isinstance(b, int) and b == 0:
                return probs[:, i * D:(i + 1) * D]
            return x_ln[:, i % 2, :]

        wo_stage = oT[:, :, 0:D]

        def res_tile(b, i):
            last = isinstance(b, int) and b == B - 1
            return (x_ln if last and i % 4 >= 2 else x_res)[:, i % 2, :]

        def out_buffers(b, i):
            if isinstance(b, int) and b == B - 1 and i % 2 == 1:
                as_tile = lambda q: q[:, 0:H * P].rearrange("p (h c) -> p h c", h=H)
                return as_tile(qT_hi), as_tile(qT_lo), qkv_ps
            return oT_tile_hi, oT_tile_lo, mix_ps

        def out_used(b, i):
            return b * NT + i - (1 if isinstance(b, int) and b == B - 1 and i > 0 else 0)

        def w1_piece(matrix, m):
            kb, c = divmod(m * W1_PIECE, INTER)
            return matrix[:, kb, c:c + W1_PIECE]

        block = ctx.enter_context(nc.Block())

        @block.sync
        def _(sp):
            def load_w1(m):
                if m == 0:
                    sp.wait_ge(qkv_done, B * STEPS)
                if m >= W1_STAGES:
                    sp.wait_ge(w1_lo_made, m - W1_STAGES + 1)
                kb, c = divmod(m * W1_PIECE, INTER)
                sp.dma_start(w1["stage"][:, m % W1_STAGES, :],
                             t["W1"][kb * P:(kb + 1) * P, c:c + W1_PIECE]).then_inc(w1_in[m % W1_STAGES], 16)

            def load_ln(b, i):
                sp.wait_ge(ln_turned, b * NT + i - 1)
                sp.dma_start(x_ln[:, i % 2, :], x_tiles[b, i]).then_inc(x_ln_in[i % 2], 16)

            def load_ln_rows(b):
                sp.wait_ge(normed, b * NT)
                sp.dma_start(row_ca[:], mod_table[b, CA, :].partition_broadcast(P)).then_inc(ln_rows_in, 16)
                sp.dma_start(row_sa[:], mod_table[b, SA, :].partition_broadcast(P)).then_inc(ln_rows_in, 16)

            def load_ga(b):
                if not (isinstance(b, int) and b == 0):
                    sp.wait_ge(gated_done, b * NT)
                sp.dma_start(row_ga[:], mod_table[b, GA, :].partition_broadcast(P)).then_inc(ga_in, 16)

            def load_last_res(i):
                if i >= 4:
                    sp.wait_ge(x_last_out[i % 4], 16)
                elif i < 2:
                    sp.wait_ge(x1_out[i], (B - 1) * (NT // 2 * 16))
                sp.dma_start(res_tile(B - 1, i), x_tiles[B - 1, i]).then_inc(x_last_in[i], 16)

            def load_res(b, i):
                if not (isinstance(b, int) and b == 0 and i < 2):
                    sp.wait_ge(x1_out[i % 2], b * (NT // 2 * 16) + i // 2 * 16)
                sp.dma_start(x_res[:, i % 2, :], x_tiles[b, i]).then_inc(x_res_in[i % 2], 16)

            def store(b, i):
                wait_alone(sp, x1_done, b * NT + i + 1, ga_in, 16)
                last = isinstance(b, int) and b == B - 1
                sp.dma_start(x1_tiles[b, i], res_tile(b, i)).then_inc(x_last_out[i % 4] if last else x1_out[i % 2], 16)

            for i in range(X_EARLY, NT):
                sp.dma_start(ln_tile(0, i), x_tiles[0, i]).then_inc(x_first_in[i], 16)
            for kb in range(KB):
                sp.dma_start(wo_stage[:, kb, :], t["wo"][kb * P:(kb + 1) * P, :]).then_inc(wo_in, 16)

            def body(b, kind, steps):
                for k in range(steps):
                    st = Step(b, k, kind)
                    if k == 1 and kind in ("first", "middle"):
                        load_ln_rows(b + 1)
                    for j in st.gate:
                        store(b - 1, j)
                        if kind == "tail" and j + 4 < NT:
                            load_last_res(j + 4)
                        if kind != "tail" and j + 2 < NT:
                            load_res(b - 1, j + 2)
                    if k == WO_STEP[-1] + 2 and kind != "tail":
                        load_ga(b)
                        if kind == "last":
                            for j in range(4):
                                load_last_res(j)
                        else:
                            load_res(b, 0)
                            load_res(b, 1)
                    t_ln = st.ln(-3)
                    if t_ln is not None:
                        load_ln(b + 1, t_ln)
                    for m in st.w1_pieces(W1_LOAD):
                        load_w1(m)

            batch_rows(sp, body)
            for j in range(2):
                sp.wait_ge(x1_out[j], 16 * (B - 1) * NT // 2)

        @block.tensor
        def _(pe):
            def three(out, a_hi, a_lo, b_hi, b_lo, start, stop):
                pe.matmul(out, a_hi, b_hi, start=start, stop=False)
                pe.matmul(out, a_hi, b_lo, start=False, stop=False)
                return pe.matmul(out, a_lo, b_hi, start=False, stop=stop)

            def project(b, h, i, kbs):
                if kbs[0] == 0:
                    pe.wait_ge(hT_lo_done, b * NT + i + 1)
                    if not (isinstance(b, int) and b == 0 and h == 0 and i == 0):
                        pe.wait_ge(nat_copied, b * STEPS + h * NT + i)
                cols = slice(i * P, (i + 1) * P)
                for kb in kbs:
                    ins = three(qkv_ps[:, 0:QKV], hT_hi[:, kb, cols], hT_lo[:, kb, cols],
                                wqkv_hi[:, kb, h, :], wqkv_lo[:, kb, h, :], kb == 0, kb == KB - 1)
                if kbs[-1] == KB - 1:
                    ins.then_inc(qkv_done, 1)

            def turn(n, i):
                pe.wait_ge(rotated, n + 1)
                if not (isinstance(n, int) and n == 0):
                    pe.wait_ge(qk_lo_done, n)
                pe.transpose(turn_ps[:, 0:P], nat[:, i % 2, 0:DH], ident[:])
                pe.transpose(turn_ps[:, P:2 * P], nat[:, i % 2, DH:2 * DH], ident[:]).then_inc(turned, 1)

            def scores(st):
                i, par = st.i, st.h % 2
                pe.wait_ge(qk_lo_done, st.n + 1)
                if not (st.kind == "first" and st.k == 0):
                    pe.wait_ge(exp_done, st.n)
                q_cols = slice(i * P, (i + 1) * P)
                for c in range(0, (i + 1) * P, 512):
                    end = min((i + 1) * P, c + 512)
                    diagonal = end == (i + 1) * P
                    ins = three(s_ps[:, c:end], qT_hi[:, q_cols], qT_lo[:, q_cols],
                                kT_hi[:, par, c:end], kT_lo[:, par, c:end], True, not diagonal)
                    if diagonal:
                        ins = pe.matmul(s_ps[:, i * P:end], w["ident16"][:], w["mask16"][:],
                                        start=False, stop=True)
                ins.then_inc(scores_done, 1)

            def transpose_probs(st, s):
                if s < CHUNKS and st.has_chunk(s):
                    group, j, _ = st.chunk(s)
                    done = (st.b * H + st.h - (1 if group == 1 else 0)) * GROUPS + group + 1
                    pe.wait_ge(probs_done, done * (GT - 1))
                    pe.wait_ge(last_probs_done, done)
                    if group == 1 and j == GT:
                        pe.wait_ge(rest_probs_done, st.b * H + st.h)
                    count = st.chunk_count(s)
                    if not (st.kind == "first" and st.h == 0 and s < NT + 2):
                        pe.wait_ge(pT_lo_done, count - 2)
                    for i in range(max(j, GT * group), GT * group + GT):
                        c = p_column(i) + j * P
                        o = (i - GT * group) * P
                        ins = pe.transpose(pT_ps[s % 2][:, o:o + P], probs[:, c:c + P], ident[:])
                    ins.then_inc(pT_done, 1)

            def attend(st, s):
                if st.has_chunk(s):
                    group, j, par = st.chunk(s)
                    pe.wait_ge(pT_lo_done, st.chunk_count(s))
                    if j == 0 and not (st.kind == "first" and st.h == 0):
                        before = st.b * (2 * H) + 2 * st.h + (0 if group == 0 else -1)
                        pe.wait_ge(oT_done, before)
                    c0 = max(0, j - GT * group) * P
                    buf = s % 2
                    three(o_ps[:, c0:], v_hi[:, par, j, :], v_lo[:, par, j, :],
                          pT_hi[:, buf, c0:], pT_lo[:, buf, c0:], j == 0,
                          j == GT * group + GT - 1).then_inc(pv_done, 1)

            def slot(st, s):
                if s == 0:
                    attend(st, -1)
                    transpose_probs(st, 0)
                else:
                    transpose_probs(st, s)
                    attend(st, s - 1)

            def turn_ln(b, i):
                pe.wait_ge(normed, b * NT + i + 1)
                if not (isinstance(b, int) and b == 0 and i == 0):
                    pe.wait_ge(hT_lo_done, b * NT + i)
                if i == 0 and not (isinstance(b, int) and b <= 1):
                    pe.wait_ge(gated_done, (b - 1) * NT)
                for kb in range(KB):
                    ins = pe.transpose(mix_ps[:, kb * P:(kb + 1) * P], ln_tile(b, i)[:, kb * P:(kb + 1) * P], ident[:])
                ins.then_inc(ln_turned, 1)

            def output(b, i):
                pe.wait_ge(oT_lo_done, b * NT + i + 1)
                if i == 0:
                    if not (isinstance(b, int) and b == B - 1):
                        pe.wait_ge(hT_lo_done, (b + 2) * NT)
                else:
                    pe.wait_ge(gated_done, out_used(b, i))
                tile_hi, tile_lo, y_ps = out_buffers(b, i)
                for h in range(H):
                    ins = three(y_ps[:], tile_hi[:, h, :], tile_lo[:, h, :],
                                wo_hi[:, h, :], wo_lo[:, h, :], h == 0, h == H - 1)
                ins.then_inc(y_done, 1)

            for i in range(NT + 1):
                if i < NT:
                    turn_ln(0, i)
                if i > 2:
                    turn(i - 3, i - 3)
                if i > 0:
                    project(0, 0, i - 1, range(KB))

            def body(b, kind, steps):
                for k in range(steps):
                    st = Step(b, k, kind)
                    i = st.i
                    nb, nh = (b + 1, 0) if st.h == H - 1 else (b, st.h + 1)
                    if kind == "tail" and k >= NT:
                        for j in st.out:
                            output(b - 1, j)
                        continue
                    if st.scores:
                        scores(st)
                    todo = chunks_of(i)
                    slot(st, todo[0])
                    if st.ln(0) is not None:
                        turn_ln(b + 1, st.ln(0))
                    if st.project:
                        project(nb, nh, i, range(0, KB // 2))
                    if st.turn:
                        turn(st.n + NT - 2, (i - 2) % NT)
                    if len(todo) > 1:
                        slot(st, todo[1])
                    if st.project:
                        project(nb, nh, i, range(KB // 2, KB))
                    for j in st.out:
                        output(b - 1, j)

            batch_rows(pe, body)

        @block.scalar
        def _(act):
            def natural(n, i):
                act.wait_ge(qkv_done, n + 1)
                if not (isinstance(n, int) and n < 2):
                    act.wait_ge(turned, n - 1)
                    act.wait_ge(v_lo_done, n - 1)
                act.activation(nat[:, i % 2, :], qkv_ps[:, 0:QKV], ACT.Copy).then_inc(nat_copied, 1)

            def v_high(n, i, par):
                act.wait_ge(nat_copied, n + 1)
                act.activation(v_hi[:, par, i, :], nat[:, i % 2, 2 * DH:QKV], ACT.Copy).then_inc(v_hi_done, 1)

            def oT_tile_hi_of(b, i):
                act.wait_ge(oT_done, b * (2 * H) + 2 * H - 1 + i // GT)
                if not (isinstance(b, int) and b == 0 and i == 0):
                    act.wait_ge(y_done, out_used(b, i))
                act.activation(out_buffers(b, i)[0][:], oT[:, :, i * P:(i + 1) * P], ACT.Copy).then_inc(oT_hi_done, 1)

            def qk_hi(n, i, par):
                act.wait_ge(turned, n + 1)
                cols = slice(i * P, (i + 1) * P)
                act.activation(qT_hi[:, cols], turn_ps[:, 0:P], ACT.Copy)
                act.activation(kT_hi[:, par, cols], turn_ps[:, P:2 * P], ACT.Copy).then_inc(qk_hi_done, 1)

            def hT_hi_of(b, i):
                act.wait_ge(ln_turned, b * NT + i + 1)
                act.activation(hT_hi[:, :, i * P:(i + 1) * P], mix_ps[:].rearrange("p (k c) -> p k c", k=KB),
                               ACT.Copy).then_inc(hT_hi_done, 1)

            def w1_high(m):
                act.wait_ge(w1_in[m % W1_STAGES], 16 * (m // W1_STAGES + 1))
                act.activation(w1_piece(w1["hi"], m), w1["stage"][:, m % W1_STAGES, :],
                               ACT.Copy).then_inc(w1_hi_made, 1)

            def pT_hi_of(st, s):
                if s < CHUNKS and st.has_chunk(s):
                    group, j, _ = st.chunk(s)
                    c0 = max(0, j - GT * group) * P
                    act.wait_ge(pT_done, st.chunk_count(s))
                    act.activation(pT_hi[:, s % 2, c0:], pT_ps[s % 2][:, c0:], ACT.Copy).then_inc(pT_hi_done, 1)

            def attended(st, s):
                if st.has_chunk(s - 1):
                    group, _, _ = st.chunk(s - 1)
                    act.wait_ge(pv_done, st.chunk_count(s - 1))
                    head = (st.h - 1) % H
                    if st.kind == "first" and head == 0:
                        act.wait_ge(wo_lo_made, 1)
                    if head == 0 and not (st.kind == "first"):
                        act.wait_ge(oT_lo_done, (st.b - 1) * NT + (group + 1) * GT)
                    act.activation(oT[:, head, group * GT * P:(group + 1) * GT * P], o_ps[:],
                                   ACT.Copy).then_inc(oT_done, 1)

            def exps(st):
                i = st.i
                W = (i + 1) * P
                act.wait_ge(max_done, st.n + 1)
                act.activation(probs[:, p_column(i):p_column(i) + W], s_ps[:, 0:W], ACT.Exp,
                               bias=neg_max[:, i:i + 1], accum_out=row_sum[:, i:i + 1]).then_inc(exp_done, 1)

            for i in range(NT + 1):
                if i < NT:
                    hT_hi_of(0, i)
                if i > 2:
                    qk_hi(i - 3, i - 3, 0)
                if i > 0:
                    natural(i - 1, i - 1)
                    v_high(i - 1, i - 1, 0)
            act.wait_ge(wo_in, 16 * KB)
            act.activation(wo_hi[:], wo_stage, ACT.Copy).then_inc(wo_hi_made, 1)

            def body(b, kind, steps):
                for k in range(steps):
                    st = Step(b, k, kind)
                    i = st.i
                    todo = chunks_of(i)
                    if st.natural:
                        natural(st.n + NT - 1, (i - 1) % NT)
                    if kind == "tail" and k > NT // 2:
                        for j in st.out:
                            oT_tile_hi_of(b - 1, j)
                        for m in st.w1_pieces(W1_SPLIT):
                            w1_high(m)
                        continue
                    for j in st.out:
                        oT_tile_hi_of(b - 1, j)
                    pT_hi_of(st, todo[0])
                    if i == 0:
                        attended(st, 0)
                    if i == NT // 2:
                        attended(st, NT)
                    if st.natural:
                        v_high(st.n + NT - 1, (i - 1) % NT, (st.h + (i > 0)) % 2)
                    if st.ln(0) is not None:
                        hT_hi_of(b + 1, st.ln(0))
                    if st.scores:
                        exps(st)
                    if st.turn:
                        qk_hi(st.n + NT - 2, (i - 2) % NT, (st.h + (i > 1)) % 2)
                    if len(todo) > 1:
                        pT_hi_of(st, todo[1])
                    for m in st.w1_pieces(W1_SPLIT):
                        w1_high(m)

            batch_rows(act, body)

        @block.vector
        def _(dve):
            def ropes(n, i):
                dve.wait_ge(nat_copied, n + 1)
                if not (isinstance(n, int) and n == 0):
                    dve.wait_ge(rotated, n)
                qk = nat[:, i % 2, 0:2 * DH].rearrange("p (t c) -> p t c", t=2)
                even, odd = slice(0, HALF), slice(HALF, ROT)

                def table(name, part):
                    return w[name][:, i:i + 1, part].to_broadcast([P, 2, part.stop - part.start])

                dve.tensor_tensor(by_cos[:], qk[:, :, 0:ROT], table("cos", slice(0, ROT)), ALU.mult)
                dve.tensor_tensor(by_sin[:, :, even], qk[:, :, odd], table("sin", even), ALU.mult)
                dve.tensor_tensor(by_sin[:, :, odd], qk[:, :, even], table("sin", odd), ALU.mult).then_inc(ropes_done, 1)

            def rotate(n, i):
                dve.wait_ge(ropes_done, n + 1)
                qk = nat[:, i % 2, 0:2 * DH].rearrange("p (t c) -> p t c", t=2)
                dve.tensor_tensor(qk[:, :, 0:ROT], by_cos[:], by_sin[:], ALU.add).then_inc(rotated, 1)

            def v_low(n, i, par):
                dve.wait_ge(v_hi_done, n + 1)
                dve.tensor_tensor(v_lo[:, par, i, :], nat[:, i % 2, 2 * DH:QKV], v_hi[:, par, i, :].bitcast(F32),
                                  ALU.subtract).then_inc(v_lo_done, 1)

            def qk_lo(n, i, par):
                dve.wait_ge(qk_hi_done, n + 1)
                cols = slice(i * P, (i + 1) * P)
                dve.tensor_tensor(qT_lo[:, cols], turn_ps[:, 0:P], qT_hi[:, cols].bitcast(F32), ALU.subtract)
                dve.tensor_tensor(kT_lo[:, par, cols], turn_ps[:, P:2 * P], kT_hi[:, par, cols].bitcast(F32),
                                  ALU.subtract).then_inc(qk_lo_done, 1)

            def hT_lo_of(b, i):
                dve.wait_ge(hT_hi_done, b * NT + i + 1)
                dve.tensor_tensor(hT_lo[:, :, i * P:(i + 1) * P], mix_ps[:].rearrange("p (k c) -> p k c", k=KB),
                                  hT_hi[:, :, i * P:(i + 1) * P].bitcast(F32), ALU.subtract).then_inc(hT_lo_done, 1)

            def pT_lo_of(st, s):
                if s < CHUNKS and st.has_chunk(s):
                    group, j, _ = st.chunk(s)
                    c0 = max(0, j - GT * group) * P
                    dve.wait_ge(pT_hi_done, st.chunk_count(s))
                    dve.tensor_tensor(pT_lo[:, s % 2, c0:], pT_ps[s % 2][:, c0:], pT_hi[:, s % 2, c0:].bitcast(F32),
                                      ALU.subtract).then_inc(pT_lo_done, 1)

            def maxima(st):
                i = st.i
                dve.wait_ge(scores_done, st.n + 1)
                dve.tensor_reduce(neg_max[:, i:i + 1], s_ps[:, 0:(i + 1) * P], AX.X, ALU.max,
                                  negate=True).then_inc(max_done, 1)

            def inverse(st):
                dve.wait_ge(exp_done, st.n + 1)
                dve.reciprocal(inv_sum[:, st.i:st.i + 1], row_sum[:, st.i:st.i + 1]).then_inc(inv_done, 1)

            def normalise(st):
                i = st.i
                dve.wait_ge(inv_done, st.n + 1)
                p = probs[:, p_column(i):p_column(i) + GT * P]
                dve.tensor_scalar(p, p, inv_sum[:, i:i + 1], None, ALU.mult).then_inc(last_probs_done, 1)

            def ln_stats(b, i):
                if isinstance(b, int) and b == 0:
                    if i >= X_EARLY:
                        dve.wait_ge(x_first_in[i], 16)
                else:
                    dve.wait_ge(x_ln_in[i % 2], (b - 1) * (NT // 2 * 16) + (i // 2 + 1) * 16)
                dve.bn_stats(stats[:, i % 2, :], ln_tile(b, i)).then_inc(bn_done, 1)
                wait_alone(dve, bn_done, b * NT + i + 1, bn_done, 1)
                dve.bn_aggr(mean_var[:, i % 2, :], stats[:, i % 2, :]).then_inc(mv_done, 1)

            def ln_apply(b, i):
                x = ln_tile(b, i)
                if i == 0 and not (isinstance(b, int) and b == 0):
                    dve.wait_ge(ln_rows_in, b * 32)
                dve.wait_ge(mv_done, b * NT + i + 1)
                dve.scalar_tensor_tensor(out=x, in0=x, scalar=mean_var[:, i % 2, 0:1], in1=row_ca[:],
                                         op0=ALU.subtract, op1=ALU.mult).then_inc(scaled, 1)
                dve.wait_ge(scaled, b * NT + i + 1)
                dve.wait_ge(rstd_done, b * NT + i + 1)
                dve.scalar_tensor_tensor(out=x, in0=x, scalar=rstd[:, i % 2, :], in1=row_sa[:],
                                         op0=ALU.mult, op1=ALU.add).then_inc(normed, 1)

            def oT_tile_lo_of(b, i):
                dve.wait_ge(oT_hi_done, b * NT + i + 1)
                tile_hi, tile_lo, _ = out_buffers(b, i)
                dve.tensor_tensor(tile_lo[:], oT[:, :, i * P:(i + 1) * P], tile_hi[:].bitcast(F32),
                                  ALU.subtract).then_inc(oT_lo_done, 1)

            def gate(b, i):
                dve.wait_ge(y_done, b * NT + i + 1)
                if i == 0:
                    dve.wait_ge(ga_in, b * 16 + 16)
                if not (isinstance(b, int) and b == 0 and i == 0):
                    dve.wait_ge(x1_done, b * NT + i)
                dve.tensor_tensor(gated[:], out_buffers(b, i)[2][:], row_ga[:], ALU.mult).then_inc(gated_done, 1)

            ln_stats(0, 0)
            ln_stats(0, 1)
            ln_apply(0, 0)
            for i in range(NT + 2):
                if i + 2 < NT:
                    ln_stats(0, i + 2)
                if i + 1 < NT:
                    ln_apply(0, i + 1)
                if i < NT:
                    hT_lo_of(0, i)
                if i > 1:
                    ropes(i - 2, i - 2)
                    v_low(i - 2, i - 2, 0)
                    rotate(i - 2, i - 2)
                if 2 < i <= NT:
                    qk_lo(i - 3, i - 3, 0)

            def body(b, kind, steps):
                for k in range(steps):
                    st = Step(b, k, kind)
                    i = st.i
                    todo = chunks_of(i)
                    if kind != "tail":
                        for j in st.gate:
                            gate(b - 1, j)
                    if st.scores:
                        maxima(st)
                    if not (kind == "tail" and k > NT // 2):
                        pT_lo_of(st, todo[0])
                    for j in st.out:
                        oT_tile_lo_of(b - 1, j)
                    if kind == "tail":
                        for j in st.gate:
                            gate(b - 1, j)
                    if st.natural:
                        ropes(st.n + NT - 1, (i - 1) % NT)
                        v_low(st.n + NT - 1, (i - 1) % NT, (st.h + (i > 0)) % 2)
                        rotate(st.n + NT - 1, (i - 1) % NT)
                    if st.scores:
                        inverse(st)
                        if i % GT == GT - 1:
                            normalise(st)
                    if st.ln(0) is not None:
                        hT_lo_of(b + 1, st.ln(0))
                    if st.turn:
                        qk_lo(st.n + NT - 2, (i - 2) % NT, (st.h + (i > 1)) % 2)
                    if len(todo) > 1 and not (kind == "tail" and k > NT // 2):
                        pT_lo_of(st, todo[1])
                    if st.ln(-1) is not None:
                        ln_apply(b + 1, st.ln(-1))
                    if st.ln(-2) is not None:
                        ln_stats(b + 1, st.ln(-2))

            batch_rows(dve, body)

        @block.gpsimd
        def _(pool):
            pool.memset(minus_half[:], -0.5).then_inc(half_set, 1)
            pool.wait_ge(half_set, 1)

            def normalise_rest(st):
                i = st.i
                wait_alone(pool, inv_done, st.n + 1, half_set, 1)
                p = probs[:, p_column(i) + GT * P:p_column(i + 1)]
                pool.tensor_scalar(p, p, inv_sum[:, i:i + 1], None, ALU.mult).then_inc(rest_probs_done, 1)

            def normalise(st):
                i = st.i
                wait_alone(pool, inv_done, st.n + 1, half_set, 1)
                p = probs[:, p_column(i):p_column(i + 1)]
                pool.tensor_scalar(p, p, inv_sum[:, i:i + 1], None, ALU.mult).then_inc(probs_done, 1)

            def inverse_deviation(b, i):
                wait_alone(pool, mv_done, b * NT + i + 1, half_set, 1)
                pool.tensor_scalar(rstd[:, i % 2, :], mean_var[:, i % 2, 1:2], EPS, None, ALU.add).then_inc(eps_done, 1)
                pool.wait_ge(eps_done, b * NT + i + 1)
                pool.tensor_tensor(rstd[:, i % 2, :], rstd[:, i % 2, :], minus_half[:], ALU.pow).then_inc(rstd_done, 1)

            def residual(b, i):
                pool.wait_ge(gated_done, b * NT + i + 1)
                if isinstance(b, int) and b == B - 1:
                    pool.wait_ge(x_last_in[i], 16)
                else:
                    pool.wait_ge(x_res_in[i % 2], b * (NT // 2 * 16) + (i // 2 + 1) * 16)
                x = res_tile(b, i)
                pool.tensor_tensor(x, x, gated[:], ALU.add).then_inc(x1_done, 1)

            def w1_low(m):
                pool.wait_ge(w1_hi_made, m + 1)
                pool.tensor_tensor(w1_piece(w1["lo"], m), w1["stage"][:, m % W1_STAGES, :],
                                   w1_piece(w1["hi"], m).bitcast(F32), ALU.subtract).then_inc(w1_lo_made, 1)

            for i in range(NT):
                inverse_deviation(0, i)
            pool.wait_ge(wo_hi_made, 1)
            pool.tensor_tensor(wo_lo[:], wo_stage, wo_hi[:].bitcast(F32), ALU.subtract).then_inc(wo_lo_made, 1)

            def body(b, kind, steps):
                for k in range(steps):
                    st = Step(b, k, kind)
                    i = st.i
                    for j in st.gate:
                        residual(b - 1, j)
                    if st.scores and i % GT < GT - 1:
                        normalise(st)
                    if st.scores and i == NT - 1:
                        normalise_rest(st)
                    t_ln = st.ln(-2)
                    if t_ln is not None:
                        inverse_deviation(b + 1, t_ln)
                    for m in st.w1_pieces(W1_SPLIT):
                        w1_low(m)

            batch_rows(pool, body)


def ffn(nc, t, mod_table, x1, out, w1, hT_hi, ident, x_last_out):
    x1_groups = x1.rearrange("b (g i p) d -> b g p i d", p=P, i=GT)
    out_groups = out.rearrange("b (g i p) d -> b g p i d", p=P, i=GT)
    N = GT * P
    LN_SLOT = [7, 9, 11, 13]

    with ExitStack() as ctx:
        def sb(name, shape, dt=F32):
            return ctx.enter_context(nc.sbuf_tensor(name, shape, dt))

        def psum(name):
            return ctx.enter_context(nc.psum_tensor(name, [P, 512], F32))

        def sem(name):
            return ctx.enter_context(nc.semaphore(name))

        w1_hi, w1_lo = w1["hi"], w1["lo"]
        w2_hi = sb("w2_hi", [P, IB, D], F32R)
        w2_lo = sb("w2_lo", [P, IB, D], F32R)
        x = sb("x1_group", [P, 2, GT, D])
        xn = sb("x1_normed", [P, 2, D])
        hT_lo = sb("h2T_lo", [P, 2, KB, N], F32R)
        relu = sb("relu", [P, 2, N])
        aT_hi = sb("aT_hi", [P, 2, N], F32R)
        aT_lo = sb("aT_lo", [P, 2, N], F32R)
        gated = sb("z_gated", [P, 2, D])
        row_cb = sb("row_cb", [P, D])
        row_sb = sb("row_sb", [P, D])
        row_gb = sb("row_gb", [P, D])
        row_b2g = sb("row_b2g", [P, D])
        b1_cols = sb("b1_cols", [P, IB])
        stats = sb("stats2", [P, 2, 6])
        mean_var = sb("mean_var2", [P, 2, 2])
        rstd = sb("rstd2", [P, 2, 1])
        minus_half = sb("minus_half2", [P, 1])

        a_ps = [psum(f"a_ps{j}") for j in range(2)]
        z_ps = [psum(f"z_ps{j}") for j in range(GT)]
        ln_ps = psum("ln_ps")

        const_in = sem("ffn_tables_loaded")
        w2_in = [sem(f"w2_stage{j}_loaded") for j in range(2)]
        w2_hi_made = sem("w2_hi_made")
        w2_made = sem("w2_split")
        x_first_in = [sem(f"x1_first{j}_loaded") for j in range(GT)]
        x_in = [sem(f"x1_{j}_loaded") for j in range(2)]
        out_done = [sem(f"out_{j}_stored") for j in range(2)]
        ln_rows_in = sem("ffn_ln_rows_loaded")
        b2g_in = sem("b2g_loaded")
        gb_in = sem("gb_loaded")
        bn_done = sem("ffn_bn_done")
        mv_done = sem("ffn_mean_var_done")
        scaled = sem("ffn_x_scaled")
        normed = sem("ffn_x_normed")
        half_set = sem("ffn_minus_half_set")
        eps_done = sem("ffn_eps_added")
        rstd_done = sem("ffn_rstd_done")
        ln_turned = sem("ffn_ln_turned")
        hT_hi_done = sem("h2T_hi_done")
        hT_lo_done = sem("h2T_lo_done")
        a_done = sem("a_done")
        relu_done = sem("relu_done")
        a_lo_done = sem("a_lo_done")
        up_used = sem("aT_used")
        z_done = sem("z_done")
        z_out = sem("z_gated_done")
        biased = sem("residual_biased")
        summed = sem("out_summed")
        last_summed = sem("last_group_summed")
        last_out_done = sem("last_group_stored")

        PIECE = GT // 2
        PIECES = IB // PIECE
        W2_SPLIT = [[2], [3], [4, 5], [6, 7]]
        w2_blocks = t["W2"].rearrange("(q i p) d -> q p i d", p=P, i=PIECE)

        def stage(m):
            return x[:, 1, m % 2 * PIECE:(m % 2 + 1) * PIECE, :]

        block = ctx.enter_context(nc.Block())

        def groups(engine, body):
            body(0, 0, "first")
            body(0, 1, "middle")
            with engine.Fori(1, B - 1) as b:
                body(b, 0, "middle")
                body(b, 1, "middle")
            body(B - 1, 0, "middle")
            body(B - 1, 1, "last")

        def after(b, g):
            return (b, 1) if g == 0 else (b + 1, 0)

        def tiles(b, g):
            return b * (GROUPS * GT) + g * GT

        @block.sync
        def _(sp):
            def load_group(b, g):
                if not (isinstance(b, int) and b == 0):
                    sp.wait_ge(out_done[g], b * 16)
                sp.dma_start(x[:, g, :, :], x1_groups[b, g]).then_inc(x_in[g], 16)

            def load_b2g(b):
                sp.dma_start(row_b2g[:], mod_table[b, B2G, :].partition_broadcast(P)).then_inc(b2g_in, 16)

            def load_ln_rows(b):
                if not (isinstance(b, int) and b == 0):
                    sp.wait_ge(normed, b * (GROUPS * GT))
                    sp.wait_ge(biased, b * (GROUPS * GT))
                for r, row in ((CB, row_cb), (SB, row_sb)):
                    sp.dma_start(row[:], mod_table[b, r, :].partition_broadcast(P)).then_inc(ln_rows_in, 16)
                load_b2g(b)

            def load_gb(b):
                if not (isinstance(b, int) and b == 0):
                    sp.wait_ge(z_out, b * (GROUPS * GT))
                sp.dma_start(row_gb[:], mod_table[b, GB, :].partition_broadcast(P)).then_inc(gb_in, 16)

            def store(b, g):
                wait_alone(sp, summed, tiles(b, g) + GT, gb_in, 16)
                sp.dma_start(out_groups[b, g], x[:, g, :, :]).then_inc(out_done[g], 16)

            for j in range(GT):
                if j == 1:
                    load_ln_rows(0)
                sp.dma_start(x[:, 0, j, :], x1_groups[0, 0][:, j, :]).then_inc(x_first_in[j], 16)
            sp.dma_start(b1_cols[:], t["b1"].rearrange("(i p) -> p i", p=P),
                         allow_slow_non_contiguous=True).then_inc(const_in, 16)
            for m in range(PIECES):
                if m >= 2:
                    sp.wait_ge(w2_made, m - 1)
                sp.dma_start(stage(m), w2_blocks[m]).then_inc(w2_in[m % 2], 16)
            load_gb(0)
            for j in range(4):
                sp.wait_ge(x_last_out[j], 16 * NT // 4)
            sp.wait_ge(w2_made, PIECES)
            load_group(0, 1)

            def body(b, g, kind):
                if kind != "first":
                    pb, pg = (b, 0) if g == 1 else (b - 1, 1)
                    store(pb, pg)
                    if g == 0:
                        load_gb(b)
                        load_group(b, 1)
                    elif not (isinstance(b, int) and b == B - 1):
                        load_group(b + 1, 0)
                if g == 0 and not (isinstance(b, int) and b == B - 1):
                    load_ln_rows(b + 1)
            groups(sp, body)
            for j in range(GT):
                sp.wait_ge(last_summed, j + 1)
                sp.dma_start(out_groups[B - 1, 1][:, j, :], x[:, 1, j, :]).then_inc(last_out_done, 16)
            sp.wait_ge(out_done[0], 16 * B)
            sp.wait_ge(out_done[1], 16 * (B - 1))
            sp.wait_ge(last_out_done, 16 * GT)

        @block.tensor
        def _(pe):
            def three(out_ps, a_hi, a_lo, b_hi, b_lo, start, stop):
                pe.matmul(out_ps, a_hi, b_hi, start=start, stop=False)
                pe.matmul(out_ps, a_hi, b_lo, start=False, stop=False)
                return pe.matmul(out_ps, a_lo, b_hi, start=False, stop=stop)

            def turn(b, g, j):
                n = tiles(b, g) + j
                pe.wait_ge(normed, n + 1)
                if not (isinstance(n, int) and n == 0):
                    pe.wait_ge(hT_lo_done, n)
                for kb in range(KB):
                    ins = pe.transpose(ln_ps[:, kb * P:(kb + 1) * P], xn[:, j % 2, kb * P:(kb + 1) * P], ident[:])
                ins.then_inc(ln_turned, 1)

            def up(b, g, i):
                n = b * (GROUPS * IB) + g * IB + i
                if i == 0:
                    pe.wait_ge(hT_lo_done, tiles(b, g) + GT)
                if not (isinstance(n, int) and n < 2):
                    pe.wait_ge(relu_done, n - 1)
                for kb in range(KB):
                    ins = three(a_ps[i % 2][:], w1_hi[:, kb, i * P:(i + 1) * P], w1_lo[:, kb, i * P:(i + 1) * P],
                                hT_hi[:, g, kb, :], hT_lo[:, g, kb, :], kb == 0, kb == KB - 1)
                ins.then_inc(a_done, 1)

            def down(b, g, i):
                n = b * (GROUPS * IB) + g * IB + i
                pe.wait_ge(a_lo_done, n + 1)
                for j in range(GT):
                    if i == 0 and not (isinstance(b, int) and b == 0 and g == 0):
                        pe.wait_ge(z_out, tiles(b, g) - GT + j + 1)
                    cols = slice(j * P, (j + 1) * P)
                    ins = three(z_ps[j][:], aT_hi[:, i % 2, cols], aT_lo[:, i % 2, cols],
                                w2_hi[:, i, :], w2_lo[:, i, :], i == 0, i == IB - 1)
                    if i == IB - 1:
                        ins.then_inc(z_done, 1)
                if i < IB - 1:
                    ins.then_inc(up_used, 1)

            for j in range(GT):
                turn(0, 0, j)

            def body(b, g, kind):
                for i in range(IB):
                    up(b, g, i)
                    if i > 0:
                        if kind == "first":
                            pe.wait_ge(w2_made, (i - 1) // PIECE + 1)
                        down(b, g, i - 1)
                    elif kind != "first":
                        pb, pg = (b, 0) if g == 1 else (b - 1, 1)
                        down(pb, pg, IB - 1)
                    if i in LN_SLOT and kind != "last":
                        turn(*after(b, g), LN_SLOT.index(i))

            groups(pe, body)
            down(B - 1, 1, IB - 1)

        @block.scalar
        def _(act):
            def hT_hi_of(b, g, j):
                act.wait_ge(ln_turned, tiles(b, g) + j + 1)
                act.activation(hT_hi[:, g, :, j * P:(j + 1) * P], ln_ps[:].rearrange("p (k c) -> p k c", k=KB),
                               ACT.Copy).then_inc(hT_hi_done, 1)

            def activate(b, g, i):
                n = b * (GROUPS * IB) + g * IB + i
                act.wait_ge(a_done, n + 1)
                if not (isinstance(n, int) and n < 2):
                    act.wait_ge(a_lo_done, n - 1)
                act.activation(relu[:, i % 2, :], a_ps[i % 2][:], ACT.Relu, bias=b1_cols[:, i:i + 1])
                act.activation(aT_hi[:, i % 2, :], a_ps[i % 2][:], ACT.Relu,
                               bias=b1_cols[:, i:i + 1]).then_inc(relu_done, 1)

            def w2_high(m):
                act.wait_ge(w2_in[m % 2], 16 * (m // 2 + 1))
                act.activation(w2_hi[:, m * PIECE:(m + 1) * PIECE, :], stage(m), ACT.Copy).then_inc(w2_hi_made, 1)

            for j in range(GT):
                hT_hi_of(0, 0, j)
            for m in range(2):
                w2_high(m)
            act.wait_ge(const_in, 16)
            for j in range(4):
                act.wait_ge(x_last_out[j], 16 * NT // 4)

            def body(b, g, kind):
                for i in range(IB):
                    activate(b, g, i)
                    if kind == "first" and i < len(W2_SPLIT):
                        for m in W2_SPLIT[i]:
                            w2_high(m)
                    if i in LN_SLOT and kind != "last":
                        hT_hi_of(*after(b, g), LN_SLOT.index(i))
            groups(act, body)

        @block.vector
        def _(dve):
            def w2_low(m):
                blocks = slice(m * PIECE, (m + 1) * PIECE)
                dve.wait_ge(w2_hi_made, m + 1)
                dve.tensor_tensor(w2_lo[:, blocks, :], stage(m), w2_hi[:, blocks, :].bitcast(F32),
                                  ALU.subtract).then_inc(w2_made, 1)

            def ln_stats(b, g, j):
                n = tiles(b, g) + j
                if isinstance(b, int) and b == 0 and g == 0:
                    dve.wait_ge(x_first_in[j], 16)
                elif j == 0:
                    dve.wait_ge(x_in[g], b * 16 + (16 if g == 1 else 0))
                dve.bn_stats(stats[:, j % 2, :], x[:, g, j, :]).then_inc(bn_done, 1)
                wait_alone(dve, bn_done, n + 1, bn_done, 1)
                dve.bn_aggr(mean_var[:, j % 2, :], stats[:, j % 2, :]).then_inc(mv_done, 1)

            def ln_apply(b, g, j):
                n = tiles(b, g) + j
                if j == 0 and g == 0:
                    dve.wait_ge(ln_rows_in, b * 32 + 32)
                dve.wait_ge(mv_done, n + 1)
                if not (isinstance(n, int) and n < 2):
                    dve.wait_ge(ln_turned, n - 1)
                dve.scalar_tensor_tensor(out=xn[:, j % 2, :], in0=x[:, g, j, :], scalar=mean_var[:, j % 2, 0:1],
                                         in1=row_cb[:], op0=ALU.subtract, op1=ALU.mult).then_inc(scaled, 1)
                dve.wait_ge(scaled, n + 1)
                dve.wait_ge(rstd_done, n + 1)
                dve.scalar_tensor_tensor(out=xn[:, j % 2, :], in0=xn[:, j % 2, :], scalar=rstd[:, j % 2, :],
                                         in1=row_sb[:], op0=ALU.mult, op1=ALU.add).then_inc(normed, 1)

            def hT_lo_of(b, g, j):
                cols = slice(j * P, (j + 1) * P)
                dve.wait_ge(hT_hi_done, tiles(b, g) + j + 1)
                dve.tensor_tensor(hT_lo[:, g, :, cols], ln_ps[:].rearrange("p (k c) -> p k c", k=KB),
                                  hT_hi[:, g, :, cols].bitcast(F32), ALU.subtract).then_inc(hT_lo_done, 1)

            def a_low(b, g, i):
                n = b * (GROUPS * IB) + g * IB + i
                dve.wait_ge(relu_done, n + 1)
                dve.tensor_tensor(aT_lo[:, i % 2, :], relu[:, i % 2, :], aT_hi[:, i % 2, :].bitcast(F32),
                                  ALU.subtract).then_inc(a_lo_done, 1)

            def gate(b, g, j):
                n = tiles(b, g) + j
                dve.wait_ge(z_done, n + 1)
                if j == 0 and g == 0:
                    dve.wait_ge(gb_in, b * 16 + 16)
                if isinstance(b, int) and b == B - 1 and g == 1:
                    if j < 2:
                        dve.wait_ge(summed, tiles(b, g))
                    else:
                        dve.wait_ge(last_summed, j - 1)
                elif not (isinstance(n, int) and n < 2):
                    dve.wait_ge(summed, n - 1)
                dve.tensor_tensor(gated[:, j % 2, :], z_ps[j][:], row_gb[:], ALU.mult).then_inc(z_out, 1)

            ln_stats(0, 0, 0)
            ln_stats(0, 0, 1)
            ln_apply(0, 0, 0)
            for j in range(GT):
                if j + 2 < GT:
                    ln_stats(0, 0, j + 2)
                if j + 1 < GT:
                    ln_apply(0, 0, j + 1)
                hT_lo_of(0, 0, j)
            for m in range(2):
                w2_low(m)

            def body(b, g, kind):
                for i in range(IB):
                    a_low(b, g, i)
                    if kind == "first" and i < len(W2_SPLIT):
                        for m in W2_SPLIT[i]:
                            w2_low(m)
                    if i == 0 and kind != "first":
                        pb, pg = (b, 0) if g == 1 else (b - 1, 1)
                        for j in range(GT):
                            gate(pb, pg, j)
                    if kind != "last":
                        if i + 2 in LN_SLOT:
                            ln_stats(*after(b, g), LN_SLOT.index(i + 2))
                        if i + 1 in LN_SLOT:
                            ln_apply(*after(b, g), LN_SLOT.index(i + 1))
                        if i in LN_SLOT:
                            hT_lo_of(*after(b, g), LN_SLOT.index(i))
            groups(dve, body)
            for j in range(GT):
                gate(B - 1, 1, j)
                dve.wait_ge(z_out, tiles(B - 1, 1) + j + 1)
                dve.wait_ge(biased, tiles(B - 1, 1) + j + 1)
                dve.tensor_tensor(x[:, 1, j, :], x[:, 1, j, :], gated[:, j % 2, :], ALU.add).then_inc(last_summed, 1)

        @block.gpsimd
        def _(pool):
            pool.memset(minus_half[:], -0.5).then_inc(half_set, 1)
            pool.wait_ge(half_set, 1)

            def inverse_deviation(b, g, j):
                n = tiles(b, g) + j
                wait_alone(pool, mv_done, n + 1, half_set, 1)
                pool.tensor_scalar(rstd[:, j % 2, :], mean_var[:, j % 2, 1:2], EPS, None, ALU.add).then_inc(eps_done, 1)
                pool.wait_ge(eps_done, n + 1)
                pool.tensor_tensor(rstd[:, j % 2, :], rstd[:, j % 2, :], minus_half[:], ALU.pow).then_inc(rstd_done, 1)

            def bias(b, g, j):
                if g == 0 and j == 0:
                    pool.wait_ge(b2g_in, b * 16 + 16)
                pool.wait_ge(normed, tiles(b, g) + j + 1)
                pool.tensor_tensor(x[:, g, j, :], x[:, g, j, :], row_b2g[:], ALU.add).then_inc(biased, 1)

            def residual(b, g, j):
                n = tiles(b, g) + j
                pool.wait_ge(z_out, n + 1)
                pool.wait_ge(biased, n + 1)
                pool.tensor_tensor(x[:, g, j, :], x[:, g, j, :], gated[:, j % 2, :], ALU.add).then_inc(summed, 1)

            for j in range(GT):
                inverse_deviation(0, 0, j)
            for j in range(GT):
                bias(0, 0, j)

            def body(b, g, kind):
                if kind != "first":
                    pb, pg = (b, 0) if g == 1 else (b - 1, 1)
                    for j in range(GT):
                        residual(pb, pg, j)
                if kind != "last":
                    for j in range(GT):
                        inverse_deviation(*after(b, g), j)
                        bias(*after(b, g), j)
            groups(pool, body)


def build(nc, t, out):
    mod_table = nc.dram_tensor("mod_table", [B, 7, D], F32, kind="Internal").ap()
    x1 = nc.dram_tensor("x1", [B, T, D], F32, kind="Internal").ap()
    with ExitStack() as outer:
        x_last_out = [outer.enter_context(nc.semaphore(f"x1_last{j}_stored")) for j in range(4)]
        word, qkv_size, hT_size, w1_size = 4, KB * H * QKV, KB * T, KB * INTER
        start = (nc.sbuf_base + 31) // 32 * 32
        outer.enter_context(nc.sbuf_tensor("region", [P, 2 * qkv_size + 2 * hT_size], F32))
        ident = outer.enter_context(nc.sbuf_tensor("ident", [P, P], F32))
        behind_w1 = 2 * w1_size
        assert behind_w1 == 2 * qkv_size + hT_size

        def placed(name, at, shape, dt=F32R):
            return nc.alloc_sbuf_tensor_at(name, shape, dt, offset=start + word * at)

        w1 = {
            "hi": placed("w1_hi", 0, [P, KB, INTER]),
            "lo": placed("w1_lo", w1_size, [P, KB, INTER]),
            "stage": placed("w1_stage", behind_w1, [P, W1_STAGES, W1_PIECE], F32),
        }
        with ExitStack() as ctx:
            def sb(name, shape, dt=F32):
                return ctx.enter_context(nc.sbuf_tensor(name, shape, dt))

            w = {
                "wqkv_hi": placed("wqkv_hi", 0, [P, KB, H, QKV]),
                "wqkv_lo": placed("wqkv_lo", qkv_size, [P, KB, H, QKV]),
                "hT_hi": placed("hT_hi", 2 * qkv_size, [P, KB, T]),
                "hT_lo": placed("hT_lo", behind_w1, [P, KB, T]),
                "wo_hi": sb("wo_hi", [P, H, D], F32R), "wo_lo": sb("wo_lo", [P, H, D], F32R),
                "stage": placed("weight_stage", 2 * qkv_size, [P, 3, KB, H, DH], F32),
                "row_ca": sb("row_ca", [P, D]), "row_sa": sb("row_sa", [P, D]),
                "probs": sb("probs", [P, p_column(NT)]),
                "cos": sb("cos", [P, NT, ROT]), "sin": sb("sin", [P, NT, ROT]), "ident": ident,
                "ident16": sb("ident16", [P, P], BF16), "mask16": sb("mask16", [P, P], BF16),
            }
            prepare(nc, t, mod_table, w)
            attention(nc, t, mod_table, x1, w, w1, x_last_out)
        hT_hi = placed("h2T_hi", behind_w1, [P, GROUPS, KB, GT * P])
        ffn(nc, t, mod_table, x1, out, w1, hT_hi, ident, x_last_out)


def tables():
    freqs = np.power(np.float32(10000.0), -np.arange(HALF, dtype=np.float32) / np.float32(HALF)).astype(np.float32)
    radians = np.arange(T, dtype=np.float32)[:, None] * freqs[None, :]
    cos, sin = np.cos(radians).astype(np.float32), np.sin(radians).astype(np.float32)
    by_tile = lambda a: np.ascontiguousarray(a.reshape(NT, P, ROT).transpose(1, 0, 2))
    upper = np.triu(np.ones((P, P), np.float32), 1)
    return {
        "cos": by_tile(np.concatenate([cos, cos], 1)), "sin": by_tile(np.concatenate([-sin, sin], 1)), "ident": np.eye(P, dtype=np.float32),
        "mask": upper * np.float32(MASKED),
    }


_NAMES = {"L0_attn_x": "x", "L0_attn_wq": "wq", "L0_attn_wk": "wk", "L0_attn_wv": "wv", "L0_attn_wo": "wo",
          "L0_ffn_W1": "W1", "L0_ffn_b1": "b1", "L0_ffn_W2": "W2", "L0_ffn_b2": "b2", "L0_c": "c", "L0_wmod": "wmod"}


def kernel(**inputs):
    import concourse.bacc as bacc
    from concourse.bass_utils import run_bass_kernel_spmd

    nc = bacc.Bacc("TRN2", target_bir_lowering=False, num_devices=1)
    arrays, t = {}, {}
    named = {short: np.ascontiguousarray(inputs[name]) for name, short in _NAMES.items()}
    for short, a in {**named, **tables()}.items():
        arrays[f"in_{short}"] = a
        t[short] = nc.dram_tensor(f"in_{short}", a.shape, mybir.dt.from_np(a.dtype), kind="ExternalInput").ap()
    out = nc.dram_tensor("out", (B, T, D), F32, kind="ExternalOutput").ap()
    build(nc, t, out)
    r = run_bass_kernel_spmd(nc, [arrays], core_ids=[0])
    return r.results[0]["out"]
```
